# Optimizing a Trainium2 kernel written in Bass

```python
import numpy as np
import jax
import jax.numpy as jnp

def _softmax(x, axis=-1):
    return jax.nn.softmax(x, axis=axis)

def _gelu(x):
    return jax.nn.gelu(x, approximate=True)

def _silu(x):
    return jax.nn.silu(x)

def _sigmoid(x):
    return jax.nn.sigmoid(x)

def _layernorm(x, axis=-1, eps=1e-05):
    m = jnp.mean(x, axis=axis, keepdims=True)
    v = jnp.var(x, axis=axis, keepdims=True)
    return (x - m) / jnp.sqrt(v + eps)

def _scatter_add(tgt, idx, src, axis=0):
    return tgt.at[idx].add(src)

def _segment_sum(src, seg, n):
    return jax.ops.segment_sum(src, seg, n)
kernel_name = 'mk_decoder_postln_d1_seqx_r2_db4401'

def setup_inputs(seed: int=0):
    np.random.seed(seed)
    _w = jnp.asarray

    def _rec_inputs():
        import jax
        import jax.numpy as jnp
        _rk = jax.random.key(seed)
        x = -0.0002928 + 1 * jax.random.normal(jax.random.fold_in(_rk, 1), (16, 256, 512), jnp.float32)
        _lenS = 256 - jax.random.randint(jax.random.fold_in(_rk, 7), (16,), 0, max(1, 256 // 4) + 1, jnp.int32)
        _lenS2 = 256 - jax.random.randint(jax.random.fold_in(_rk, 8), (16,), 0, max(1, 256 // 4) + 1, jnp.int32)
        _ctx_1024P = jax.random.normal(jax.random.fold_in(_rk, 11), (16, 16, 512), jnp.float32)
        _ctx_1024c = jax.random.dirichlet(jax.random.fold_in(_rk, 511), 0.3 * jnp.ones((16,), jnp.float32), (16, 256))
        _ctx_1024t = jnp.einsum('bsk,bkd->bsd', _ctx_1024c, _ctx_1024P)
        _ctx_1024t = _ctx_1024t * jax.lax.rsqrt(jnp.mean(jnp.square(_ctx_1024t)) + 1e-12) * 0.953939
        ctx_1024 = -1.39393e-06 + 0.999914 * (_ctx_1024t + 0.3 * jax.random.normal(jax.random.fold_in(_rk, 611), (16, 256, 512), jnp.float32))
        return (x, ctx_1024)
    x, ctx_1024 = _rec_inputs()

    def _L0_attn_setup():
        import jax, jax.numpy as jnp
        import numpy as np
        D_MODEL = 512
        NUM_HEADS = 16
        D_HEAD = D_MODEL // NUM_HEADS
        LN_EPS = 1e-05

        def apply_rope(x):
            L = x.shape[2]
            inv_freq = 1.0 / 10000.0 ** (jnp.arange(0, D_HEAD, 2, dtype=jnp.float32) / D_HEAD)
            freqs = jnp.arange(L, dtype=jnp.float32)[:, None] * inv_freq[None, :]
            sin = jnp.sin(freqs)[None, None]
            cos = jnp.cos(freqs)[None, None]
            x1 = x[..., ::2]
            x2 = x[..., 1::2]
            rot = jnp.stack([x1 * cos - x2 * sin, x1 * sin + x2 * cos], axis=-1)
            return rot.reshape(x.shape)
        key = jax.random.key(seed)
        ks = jax.random.split(key, 10)
        B, L = (4, 1024)
        s = 1.0 / np.sqrt(D_MODEL)
        inp = {'x': jax.random.normal(ks[0], (B, L, D_MODEL), dtype=jnp.float32), 'ln_gamma': jnp.ones((D_MODEL,), jnp.float32), 'ln_beta': jnp.zeros((D_MODEL,), jnp.float32), 'Wq': jax.random.normal(ks[1], (D_MODEL, D_MODEL), jnp.float32) * s, 'bq': jnp.zeros((D_MODEL,), jnp.float32), 'Wk': jax.random.normal(ks[2], (D_MODEL, D_MODEL), jnp.float32) * s, 'bk': jnp.zeros((D_MODEL,), jnp.float32), 'Wv': jax.random.normal(ks[3], (D_MODEL, D_MODEL), jnp.float32) * s, 'bv': jnp.zeros((D_MODEL,), jnp.float32), 'Wo': jax.random.normal(ks[4], (D_MODEL, D_MODEL), jnp.float32) * s, 'bo': jnp.zeros((D_MODEL,), jnp.float32)}
        return inp
    _L0_attn_all = _L0_attn_setup()
    _L0_attn_in = {k: v for k, v in _L0_attn_all.items() if k in ('ln_gamma', 'ln_beta', 'Wq', 'bq', 'Wk', 'bk', 'Wv', 'bv', 'Wo', 'bo')}
    del _L0_attn_all

    def _L0_xattn_setup():
        import jax, jax.numpy as jnp
        import numpy as np
        B, S, D = (1, 2048, 512)
        NUM_HEADS, HEAD_DIM = (16, 64)
        WINDOW = 128
        EMBED = NUM_HEADS * HEAD_DIM
        key = jax.random.key(seed)
        ks = jax.random.split(key, 7)
        scale_in = 1.0 / np.sqrt(D)
        scale_e = 1.0 / np.sqrt(EMBED)
        return {'query': jax.random.normal(ks[0], (B, S, D), dtype=jnp.float32), 'key': jax.random.normal(ks[1], (B, S, D), dtype=jnp.float32), 'value': jax.random.normal(ks[2], (B, S, D), dtype=jnp.float32), 'Wq': jax.random.normal(ks[3], (D, EMBED), dtype=jnp.float32) * scale_in, 'Wk': jax.random.normal(ks[4], (D, EMBED), dtype=jnp.float32) * scale_in, 'Wv': jax.random.normal(ks[5], (D, EMBED), dtype=jnp.float32) * scale_in, 'Wo': jax.random.normal(ks[6], (EMBED, D), dtype=jnp.float32) * scale_e}
    _L0_xattn_all = _L0_xattn_setup()
    _L0_xattn_in = {k: v for k, v in _L0_xattn_all.items() if k in ('Wq', 'Wk', 'Wv', 'Wo')}
    del _L0_xattn_all

    def _L0_ffn_setup():
        import jax, jax.numpy as jnp
        import numpy as np
        B, T, D, F_FF, E, K = (8, 1024, 512, 2048, 8, 2)
        key = jax.random.key(seed)
        ks = jax.random.split(key, 6)
        s = 1.0 / np.sqrt(D)
        return {'x': jax.random.normal(ks[0], (B, T, D), jnp.float32), 'Wr': jax.random.normal(ks[1], (D, E), jnp.float32) * s, 'W1': jax.random.normal(ks[2], (E, D, F_FF), jnp.float32) * s, 'b1': jax.random.normal(ks[3], (E, F_FF), jnp.float32) * 0.01, 'W2': jax.random.normal(ks[4], (E, F_FF, D), jnp.float32) * (1.0 / np.sqrt(F_FF)), 'b2': jax.random.normal(ks[5], (E, D), jnp.float32) * 0.01}
    _L0_ffn_all = _L0_ffn_setup()
    _L0_ffn_in = {k: v for k, v in _L0_ffn_all.items() if k in ('Wr', 'W1', 'b1', 'W2', 'b2')}
    del _L0_ffn_all
    return {'x': x, 'ctx_1024': ctx_1024, 'L0_attn_ln_gamma': _L0_attn_in['ln_gamma'], 'L0_attn_ln_beta': _L0_attn_in['ln_beta'], 'L0_attn_Wq': _L0_attn_in['Wq'], 'L0_attn_bq': _L0_attn_in['bq'], 'L0_attn_Wk': _L0_attn_in['Wk'], 'L0_attn_bk': _L0_attn_in['bk'], 'L0_attn_Wv': _L0_attn_in['Wv'], 'L0_attn_bv': _L0_attn_in['bv'], 'L0_attn_Wo': _L0_attn_in['Wo'], 'L0_attn_bo': _L0_attn_in['bo'], 'L0_xattn_Wq': _L0_xattn_in['Wq'], 'L0_xattn_Wk': _L0_xattn_in['Wk'], 'L0_xattn_Wv': _L0_xattn_in['Wv'], 'L0_xattn_Wo': _L0_xattn_in['Wo'], 'L0_ffn_Wr': _L0_ffn_in['Wr'], 'L0_ffn_W1': _L0_ffn_in['W1'], 'L0_ffn_b1': _L0_ffn_in['b1'], 'L0_ffn_W2': _L0_ffn_in['W2'], 'L0_ffn_b2': _L0_ffn_in['b2']}

def reference(x, ctx_1024, L0_attn_ln_gamma, L0_attn_ln_beta, L0_attn_Wq, L0_attn_bq, L0_attn_Wk, L0_attn_bk, L0_attn_Wv, L0_attn_bv, L0_attn_Wo, L0_attn_bo, L0_xattn_Wq, L0_xattn_Wk, L0_xattn_Wv, L0_xattn_Wo, L0_ffn_Wr, L0_ffn_W1, L0_ffn_b1, L0_ffn_W2, L0_ffn_b2):
    import jax
    import jax.numpy as jnp

    def _L0_attn_ref(x, ln_gamma, ln_beta, Wq, bq, Wk, bk, Wv, bv, Wo, bo):
        import jax, jax.numpy as jnp
        import numpy as np
        D_MODEL = 512
        NUM_HEADS = 16
        D_HEAD = D_MODEL // NUM_HEADS
        LN_EPS = 1e-05

        def apply_rope(x):
            L = x.shape[2]
            inv_freq = 1.0 / 10000.0 ** (jnp.arange(0, D_HEAD, 2, dtype=jnp.float32) / D_HEAD)
            freqs = jnp.arange(L, dtype=jnp.float32)[:, None] * inv_freq[None, :]
            sin = jnp.sin(freqs)[None, None]
            cos = jnp.cos(freqs)[None, None]
            x1 = x[..., ::2]
            x2 = x[..., 1::2]
            rot = jnp.stack([x1 * cos - x2 * sin, x1 * sin + x2 * cos], axis=-1)
            return rot.reshape(x.shape)
        B, L, _ = x.shape
        mu = jnp.mean(x, axis=-1, keepdims=True)
        var = jnp.mean(jnp.square(x - mu), axis=-1, keepdims=True)
        xn = (x - mu) * jax.lax.rsqrt(var + LN_EPS) * ln_gamma + ln_beta

        def heads(t):
            return t.reshape(B, L, NUM_HEADS, D_HEAD).transpose(0, 2, 1, 3)
        q = heads(xn @ Wq + bq)
        k = heads(xn @ Wk + bk)
        v = heads(xn @ Wv + bv)
        q = apply_rope(q)
        k = apply_rope(k)
        scores = jnp.einsum('bhid,bhjd->bhij', q, k) / jnp.sqrt(jnp.float32(D_HEAD))
        mask = jnp.tril(jnp.ones((L, L), jnp.float32))[None, None]
        scores = scores * mask + (1.0 - mask) * -1000000000.0
        probs = jax.nn.softmax(scores, axis=-1)
        out = jnp.einsum('bhij,bhjd->bhid', probs, v)
        out = out.transpose(0, 2, 1, 3).reshape(B, L, D_MODEL)
        out = out @ Wo + bo
        return x + out

    def _L0_xattn_ref(query, key, value, Wq, Wk, Wv, Wo):
        import jax, jax.numpy as jnp
        import numpy as np
        B, S, D = (1, 2048, 512)
        NUM_HEADS, HEAD_DIM = (16, 64)
        WINDOW = 128
        EMBED = NUM_HEADS * HEAD_DIM
        Bq, Sq, _ = query.shape
        q = (query @ Wq).reshape(Bq, Sq, NUM_HEADS, HEAD_DIM).transpose(0, 2, 1, 3)
        k = (key @ Wk).reshape(Bq, Sq, NUM_HEADS, HEAD_DIM).transpose(0, 2, 1, 3)
        v = (value @ Wv).reshape(Bq, Sq, NUM_HEADS, HEAD_DIM).transpose(0, 2, 1, 3)
        idx = jnp.arange(Sq)
        local_mask = jnp.abs(idx[:, None] - idx[None, :]) > WINDOW
        scores = jnp.einsum('bhqd,bhkd->bhqk', q, k) / jnp.sqrt(jnp.float32(HEAD_DIM))
        scores = jnp.where(local_mask, -jnp.inf, scores)
        attn = jax.nn.softmax(scores, axis=-1)
        out = jnp.einsum('bhqk,bhkd->bhqd', attn, v)
        out = out.transpose(0, 2, 1, 3).reshape(Bq, Sq, EMBED)
        return out @ Wo

    def _L0_ffn_ref(x, Wr, W1, b1, W2, b2):
        import jax, jax.numpy as jnp
        import numpy as np
        B, T, D, F_FF, E, K = (8, 1024, 512, 2048, 8, 2)
        pooled = x.mean(axis=1)
        logits = pooled @ Wr
        top_scores, top_idx = jax.lax.top_k(logits, K)
        weights = jax.nn.softmax(top_scores, axis=-1)
        W1s, b1s = (W1[top_idx], b1[top_idx])
        W2s, b2s = (W2[top_idx], b2[top_idx])
        h = jnp.einsum('btd,bkdf->bktf', x, W1s) + b1s[:, :, None, :]
        h = jax.nn.gelu(h, approximate=False)
        y = jnp.einsum('bktf,bkfd->bktd', h, W2s) + b2s[:, :, None, :]
        out = jnp.einsum('bk,bktd->btd', weights, y)
        return out
    x = _layernorm(x + _L0_attn_ref(x, L0_attn_ln_gamma, L0_attn_ln_beta, L0_attn_Wq, L0_attn_bq, L0_attn_Wk, L0_attn_bk, L0_attn_Wv, L0_attn_bv, L0_attn_Wo, L0_attn_bo), axis=-1)
    x = _layernorm(x + _L0_xattn_ref(x, ctx_1024, ctx_1024, L0_xattn_Wq, L0_xattn_Wk, L0_xattn_Wv, L0_xattn_Wo), axis=-1)
    x = _layernorm(x + _L0_ffn_ref(x, L0_ffn_Wr, L0_ffn_W1, L0_ffn_b1, L0_ffn_W2, L0_ffn_b2), axis=-1)
    return x

_drawn_inputs = setup_inputs


def setup_inputs(seed=0):
    import zlib

    import numpy as np

    out = dict(_drawn_inputs(seed))
    spreads = {'L0_attn_ln_gamma': (1.0, 0.2),
     'L0_attn_ln_beta': (0.0, 0.1),
     'L0_attn_bq': (0.0, 0.8),
     'L0_attn_bk': (0.0, 0.8),
     'L0_attn_bv': (0.0, 0.1),
     'L0_attn_bo': (0.0, 0.1)}
    factors = {'L0_ffn_b1': 8.0, 'L0_ffn_b2': 8.0}
    for name, (base, spread) in spreads.items():
        noise = np.random.default_rng([zlib.crc32(name.encode()), seed]).standard_normal(out[name].shape)
        drawn = base * np.exp(spread * noise) if base else spread * noise
        out[name] = jnp.asarray(drawn.astype(out[name].dtype))
    for name, factor in factors.items():
        out[name] = (out[name] * factor).astype(out[name].dtype)
    return out
```

```python
from contextlib import ExitStack

import concourse.bass as bass
from concourse import mybir

P = 128
F32 = mybir.dt.float32
F32R = mybir.dt.float32r
BF16 = mybir.dt.bfloat16
I32 = mybir.dt.int32
ALU = mybir.AluOpType
ACT = mybir.ActivationFunctionType
AX = mybir.AxisListType
EPS = 1e-5
MASKED = -1e30

B, L, D = 16, 256, 512
T = L // P
KT = D // P
HEADS = 16
E = 8
FF = 2048
SLOTS = 2 * B


def fp(ap):
    return ap.bitcast(F32)


def product3(pe, out, stationary, moving, first, last):
    (sh, sl), (mh, ml) = stationary, moving
    pe.matmul(out, sh, mh, start=first, stop=False)
    pe.matmul(out, sh, ml, start=False, stop=False)
    return pe.matmul(out, sl, mh, start=False, stop=last)


class OwnSteps:

    def __init__(self, base=0):
        self.base, self.n = base, 0

    def next(self):
        self.n += 1
        return self.base + self.n


def stand(eng, sem, value, stood):
    eng.wait_ge(sem, value)
    eng.sem_inc(stood, 1)



D1 = D // HEADS

UNITS1 = []
for _g in range(4):
    UNITS1 += [(0, list(range(4 * _g, 4 * _g + 4)), _g), (1, [4 * _g, 4 * _g + 1], _g), (1, [4 * _g + 2, 4 * _g + 3], _g)]
NU1 = len(UNITS1)

ORDER1 = [("S", 0), ("nstat",), ("pot", 0), ("S", 1), ("T", 0), ("nnorm",), ("pot", 1),
          ("S", 2), ("T", 1), ("V", 0), ("py", 0), ("nz",), ("S", 3), ("T", 2), ("V", 1), ("nproj", 0),
          ("S", 4), ("T", 3), ("V", 2), ("nproj", 1), ("S", 5), ("T", 4), ("V", 3), ("nproj", 2), ("nstack", 0),
          ("S", 6), ("T", 5), ("V", 4), ("nproj", 3), ("nstack", 1), ("S", 7), ("T", 6), ("V", 5), ("py", 1), ("nstack", 2),
          ("S", 8), ("T", 7), ("V", 6), ("nstack", 3), ("S", 9), ("T", 8), ("V", 7), ("pnorm",), ("nturn", 0),
          ("S", 10), ("T", 9), ("V", 8), ("nturn", 1), ("S", 11), ("T", 10), ("V", 9), ("nturn", 2),
          ("T", 11), ("V", 10), ("nturn", 3), ("V", 11), ("base",), ("nval", 0), ("nval", 1)]
FIRST1 = [("nstat",), ("nnorm",), ("nz",), ("nproj", 0), ("nproj", 1), ("nstack", 0), ("nproj", 2), ("nstack", 1), ("nproj", 3),
          ("nstack", 2), ("nstack", 3), ("nturn", 0), ("nturn", 1), ("nturn", 2), ("nturn", 3), ("nval", 0), ("nval", 1)]
LAST1 = [st for st in ORDER1 if not st[0].startswith("n")]
FINISH1 = [("pot", 0), ("pot", 1), ("py", 0), ("py", 1), ("pnorm",)]


class SpareBanks:

    def __init__(self, ready, by_dve, by_act):
        self.ready, self.n = ready, 0
        self.made = {"dve": by_dve, "act": by_act}
        self.past = [("dve", by_dve - 1), ("dve", by_dve)]

    def next(self, by):
        bank, before = self.n % 2, self.past[self.n]
        self.n += 1
        self.made[by] = self.made[by] + 1
        self.past.append((by, self.made[by]))
        return bank, self.ready + self.n, before


def self_attention(nc, x, gamma, beta, weights, biases, rope, x1):
    with ExitStack() as ctx:
        def sb(name, shape, dt=F32):
            return ctx.enter_context(nc.sbuf_tensor(name, shape, dt))

        def sem(name):
            return ctx.enter_context(nc.semaphore(name))

        def banks(name, n):
            return [ctx.enter_context(nc.psum_tensor(f"{name}{i}", [P, 512], F32)) for i in range(n)]

        wh = [sb(f"a_wh{i}", [P, KT, D], F32R) for i in range(4)]
        wl = [sb(f"a_wl{i}", [P, KT, D], F32R) for i in range(4)]
        bias = [sb(f"a_bias{i}", [P, D]) for i in range(4)]
        ident = sb("a_ident", [P, P])
        identb = sb("a_identb", [P, P], BF16)
        causal = sb("a_causal", [P, P], BF16)
        tables = sb("a_rope", [P, 2, 2, T, D1])
        half = sb("a_half", [P, T])
        acc = sb("a_acc", [P, T, D])
        o = sb("a_o", [P, T, D])

        S_ps, T_ps, O_ps, F_ps = banks("a_S", 2), banks("a_T", 2), banks("a_O", 2), banks("a_F", 2)

        with ExitStack() as sctx:
            raw = [sctx.enter_context(nc.sbuf_tensor(f"a_raw{i}", [P, KT, D], F32)) for i in range(4)]
            scaled = [sctx.enter_context(nc.sbuf_tensor(f"a_scaled{i}", [P, KT, D], F32)) for i in range(3)]
            gcol = sctx.enter_context(nc.sbuf_tensor("a_gcol", [P, KT], F32))
            bcol = sctx.enter_context(nc.sbuf_tensor("a_bcol", [P, KT], F32))
            brep = sctx.enter_context(nc.sbuf_tensor("a_brep", [P, KT, P], F32))
            w_in = [sctx.enter_context(nc.semaphore(f"a_w_in{i}")) for i in range(4)]
            small_in = sctx.enter_context(nc.semaphore("a_small_in"))
            made = sctx.enter_context(nc.semaphore("a_made"))
            w_scaled = sctx.enter_context(nc.semaphore("a_w_scaled"))
            w_hi = sctx.enter_context(nc.semaphore("a_w_hi"))
            rep_ready = sctx.enter_context(nc.semaphore("a_rep_ready"))
            bw_ready = sctx.enter_context(nc.semaphore("a_bw_ready"))
            block = sctx.enter_context(nc.Block())

            @block.sync
            def _(sp):
                with nc.allow_non_contiguous_dma("gamma and beta as columns, once"):
                    sp.dma_start(gcol[:, :], gamma.rearrange("(t p) -> p t", p=P)).then_inc(small_in, 16)
                    sp.dma_start(bcol[:, :], beta.rearrange("(t p) -> p t", p=P)).then_inc(small_in, 16)
                for i in range(4):
                    sp.dma_start(raw[i][:, :, :], weights[i].rearrange("(t p) n -> p t n", p=P)).then_inc(w_in[i], 16)
                for i in range(4):
                    sp.dma_start(bias[i][:, :], biases[i].partition_broadcast(P)).then_inc(small_in, 16)
                sp.dma_start(tables[:, :, :, :, :], rope).then_inc(small_in, 16)
                sp.wait_ge(small_in, 16 * 7)

            @block.gpsimd
            def _(pool):
                pool.memset(ident[:, :], 0.0).then_inc(made, 1)
                pool.memset(identb[:, :], 0.0).then_inc(made, 1)
                pool.memset(causal[:, :], 0.0).then_inc(made, 1)
                pool.memset(half[:, :], -0.5)
                pool.memset(acc[:, :, :], 0.0)
                pool.memset(o[:, :, :], 0.0)
                pool.wait_ge(made, 3)
                pool.affine_select(ident[:, :], ident[:, :], [[-1, P]], ALU.not_equal, 1.0, base=0, channel_multiplier=1)
                pool.affine_select(identb[:, :], identb[:, :], [[-1, P]], ALU.not_equal, 1.0, base=0, channel_multiplier=1)
                pool.affine_select(causal[:, :], causal[:, :], [[-1, P]], ALU.is_ge, MASKED, base=0, channel_multiplier=1)

            @block.vector
            def _(dve):
                dve.wait_ge(small_in, 16 * 7)
                dve.tensor_copy(brep[:, :, :], bcol[:, :].unsqueeze(2).to_broadcast([P, KT, P])).then_inc(rep_ready, 1)
                for i in range(4):
                    full = raw[i] if i == 3 else scaled[i]
                    dve.wait_ge(w_in[i], 16)
                    if i < 3:
                        for t in range(KT):
                            last = dve.tensor_scalar(full[:, t, :], raw[i][:, t, :], gcol[:, t:t + 1], None, ALU.mult)
                        last.then_inc(w_scaled, 1)
                    dve.wait_ge(w_hi, i + 1)
                    dve.tensor_tensor(wl[i][:, :, :], full[:, :, :], fp(wh[i][:, :, :]), ALU.subtract)
                    if i == 3:
                        dve.tensor_scalar(bias[3][:, :], bias[3][:, :], 0.5, None, ALU.mult)
                    if i < 3:
                        dve.wait_ge(bw_ready, i + 1)
                        dve.tensor_tensor(bias[i][:, :], (F_ps[0], F_ps[1], S_ps[0])[i][:, :], bias[i][:, :], ALU.add)

            @block.scalar
            def _(act):
                for i in range(4):
                    act.wait_ge(w_in[i], 16)
                    if i < 3:
                        act.wait_ge(w_scaled, i + 1)
                    act.activation(wh[i][:, :, :], (raw[i] if i == 3 else scaled[i])[:, :, :], ACT.Copy).then_inc(w_hi, 1)

            @block.tensor
            def _(pe):
                pe.wait_ge(rep_ready, 1)
                for i in range(3):
                    pe.wait_ge(w_in[i], 16)
                    bank = (F_ps[0], F_ps[1], S_ps[0])[i]
                    for t in range(KT):
                        last = pe.matmul(bank[:, :], brep[:, t, :], raw[i][:, t, :], start=t == 0, stop=t == KT - 1)
                    last.then_inc(bw_ready, 1)

        xs = sb("a_xs", [P, T, D])
        zh, zl = sb("a_zh", [P, KT, L], F32R), sb("a_zl", [P, KT, L], F32R)
        biased = [sb(f"a_biased{i}", [P, D]) for i in range(2)]
        turn_cos, turn_sin = sb("a_turn_cos", [P, D]), sb("a_turn_sin", [P, D])
        turned = [sb(f"a_turned{i}", [P, D]) for i in range(2)]
        stack = [[sb(f"a_stack{i}{t}", [P, HEADS, 4, D1], F32R) for t in range(T)] for i in range(2)]
        stackT = [sb(f"a_stackT{i}", [P, HEADS, L], F32R) for i in range(2)]
        v = [sb(f"a_v{t}", [P, HEADS, 2, D1], F32R) for t in range(T)]
        vfull = sb("a_vfull", [P, D])
        negmax = sb("a_negmax", [P, 2, 4])
        probs = [sb(f"a_probs{i}", [P, 512]) for i in range(2)]
        sums = sb("a_sums", [P, T, HEADS])
        pTh = [sb(f"a_pTh{i}", [P, 4, P], F32R) for i in range(2)]
        pTl = [sb(f"a_pTl{i}", [P, 4, P], F32R) for i in range(2)]
        rsum = sb("a_rsum", [P, T, 4])
        osum = sb("a_osum", [P, T, 4, D1])
        oTh = [sb(f"a_oTh{t}", [P, KT, P], F32R) for t in range(T)]
        oTl = [sb(f"a_oTl{t}", [P, KT, P], F32R) for t in range(T)]
        bn = sb("a_bn", [P, 2, T, 6])
        mv = sb("a_mv", [P, 2, T, 2])
        ve = sb("a_ve", [P, 2, T])
        rstd = sb("a_rstd", [P, 2, T])

        names = ["xs_in", "acc_in", "out_done", "stat", "rstd_ready", "z_ready", "f_ready", "f_dve", "f_act", "z_hi",
                 "turned_ready", "turned_hi", "turned_lo", "stacked", "v_full", "v_hi",
                 "s_ready", "max_ready", "exp_done", "t_ready", "p_hi", "p_lo", "pv_done", "o_ready",
                 "ot_hi", "base_ready", "stat2", "rstd2_ready", "out_ready", "own_dve", "own_pool", "stood"]
        s = {n: sem("a_" + n) for n in names}
        block = ctx.enter_context(nc.Block())

        def spare(b):
            return SpareBanks(24 + 28 * b, 8 + 12 * b, 16 + 16 * b)

        def spare_first():
            return SpareBanks(0, 0, 0)

        def spare_last():
            return SpareBanks(24 + 28 * (B - 1) + 4, 8 + 12 * (B - 1) + 4, 0)

        def wait_spare(eng, before, first):
            by, count = before
            if not (first and isinstance(count, int) and count <= 0):
                eng.wait_ge(s["f_" + by], count)

        def spare_uses(step):
            return {"nz": (T, "dve"), "nproj": (1, "dve"), "nturn": (4, "act"), "nval": (1, "dve"),
                    "pot": (1, "dve"), "py": (1, "dve")}.get(step, (0, "dve"))

        @block.sync
        def _(sp):
            def load_xs(b, transposed):
                if transposed is not None:
                    sp.wait_ge(s["f_ready"], transposed)
                sp.dma_start(xs[:, :, :], x[b].rearrange("(t p) d -> p t d", p=P)).then_inc(s["xs_in"], 16)

            def store(b):
                sp.wait_ge(s["out_ready"], b + 2)
                sp.dma_start(x1[b + 1].rearrange("(t p) d -> p t d", p=P), acc[:, :, :]).then_inc(s["out_done"], 16)

            def load_acc(b):
                sp.wait_ge(s["out_done"], 16 * (b + 1))
                sp.dma_start(acc[:, :, :], x[b].rearrange("(t p) d -> p t d", p=P)).then_inc(s["acc_in"], 16)

            load_xs(0, None)
            load_xs(1, T)
            with sp.Fori(0, B - 2) as b:
                load_xs(b + 2, 24 + 28 * b + 5)
                store(b - 1)
                load_acc(b)
            for b in (B - 2, B - 1):
                store(b - 1)
                load_acc(b)
            store(B - 1)
            sp.wait_ge(s["out_done"], 16 * (B + 1))

        @block.gpsimd
        def _(pool):
            pool.sem_inc(s["turned_ready"], 2)
            pool.sem_inc(s["base_ready"], 1)

            def rsqrt(own, which, ready):
                pool.tensor_scalar(ve[:, which, :], mv[:, which, :, 1], EPS, None, ALU.add).then_inc(s["own_pool"], 1)
                pool.wait_ge(s["own_pool"], own.next())
                pool.tensor_tensor(rstd[:, which, :], ve[:, which, :], half[:, :], ALU.pow).then_inc(ready, 1)

            def turn(own, by_dve, n, i):
                t, w = i // 2, i % 2
                b4 = biased[i % 2][:, :].rearrange("p (h m e) -> p h m e", h=HEADS, e=2)
                sn = turn_sin[:, :].rearrange("p (h m e) -> p h m e", h=HEADS, e=2)
                cos = tables[:, w, 0, t, :].unsqueeze(1).to_broadcast([P, HEADS, D1])
                sin = tables[:, w, 1, t, :].rearrange("p (m e) -> p m e", e=2)
                pool.wait_ge(s["f_dve"], by_dve)
                pool.wait_ge(s["turned_ready"], n + 1)
                pool.tensor_tensor(turn_cos[:, :].rearrange("p (h d) -> p h d", h=HEADS),
                                   biased[i % 2][:, :].rearrange("p (h d) -> p h d", h=HEADS), cos, ALU.mult)
                for e in range(2):
                    last = pool.tensor_tensor(sn[:, :, :, e], b4[:, :, :, 1 - e],
                                              sin[:, :, e].unsqueeze(1).to_broadcast([P, HEADS, D1 // 2]), ALU.mult)
                last.then_inc(s["own_pool"], 1)
                pool.wait_ge(s["turned_lo"], n)
                pool.wait_ge(s["own_pool"], own.next())
                pool.tensor_tensor(turned[i % 2][:, :], turn_cos[:, :], turn_sin[:, :], ALU.add).then_inc(s["turned_ready"], 1)

            def second_lo(n, i):
                t, w = i // 2, i % 2
                stand(pool, s["turned_lo"], n + 2, s["stood"])
                a, c = (2, 3) if w == 0 else (1, 3)
                pool.tensor_copy(stack[w][t][:, :, c, :], fp(stack[w][t][:, :, a, :])).then_inc(s["stacked"], 1)

            def body(b, order, by_dve, own):
                for step in order:
                    if step[0] == "nstat":
                        stand(pool, s["stat"], b + 2, s["stood"])
                        rsqrt(own, 0, s["rstd_ready"])
                    elif step[0] == "nproj":
                        i = step[1]
                        turn(own, by_dve + i, 4 * (b + 1) + i + 1, i)
                    elif step[0] == "nstack":
                        second_lo(4 * (b + 1) + step[1] + 1, step[1])
                    elif step == ("py", T - 1):
                        stand(pool, s["stat2"], b + 1, s["stood"])
                        rsqrt(own, 1, s["rstd2_ready"])
                    elif step[0] == "base":
                        pool.wait_ge(s["acc_in"], 16 * (b + 1))
                        pool.tensor_tensor(acc[:, :, :], acc[:, :, :], bias[3][:, :].unsqueeze(1).to_broadcast([P, T, D]),
                                           ALU.add).then_inc(s["base_ready"], 1)

            per_body = 1 + 4 + 1
            body(-1, FIRST1, T + 1, OwnSteps())
            with pool.Fori(0, B - 1) as b:
                body(b, ORDER1, 8 + 12 * b + 6, OwnSteps(5 + per_body * b))
            body(B - 1, LAST1, None, OwnSteps(5 + per_body * (B - 1)))
            body(B, FINISH1, None, OwnSteps(5 + per_body * (B - 1) + 1))

        @block.scalar
        def _(act):
            act.sem_inc(s["exp_done"], 2)

            def body(b, order, ring):
                u0 = NU1 * b
                for step in order:
                    n, by = spare_uses(step[0])
                    uses = [ring.next(by) for _ in range(n)]
                    if step[0] == "S":
                        u = step[1]
                        t, heads, g = UNITS1[u]
                        act.wait_ge(s["max_ready"], u0 + u + 1)
                        act.wait_ge(s["t_ready"], u0 + u + 1)
                        nj = P * (t + 1)
                        for j, h in enumerate(heads):
                            last = act.activation(probs[u % 2][:, j * nj:(j + 1) * nj], S_ps[u % 2][:, j * nj:(j + 1) * nj],
                                                  ACT.Exp, bias=negmax[:, u % 2, j:j + 1], accum_out=sums[:, t, h:h + 1])
                        last.then_inc(s["exp_done"], 1)
                    elif step[0] == "T":
                        u = step[1]
                        act.wait_ge(s["t_ready"], u0 + u + 3)
                        act.wait_ge(s["pv_done"], u0 + u + 1)
                        act.activation(pTh[u % 2][:, :, :], T_ps[u % 2][:, :], ACT.Copy).then_inc(s["p_hi"], 1)
                    elif step[0] == "nz":
                        for j, (bank, ready, _) in enumerate(uses):
                            act.wait_ge(s["f_ready"], ready)
                            act.activation(zh[:, 2 * j:2 * j + 2, :], F_ps[bank][:, :], ACT.Copy).then_inc(s["z_hi"], 1)
                    elif step[0] == "nstack":
                        i = step[1]
                        w, t = i % 2, i // 2
                        act.wait_ge(s["turned_ready"], 4 * (b + 1) + i + 3)
                        places = stack[w][t][:, :, 0:2, :] if w == 0 else stack[w][t][:, :, 0:4:2, :]
                        act.activation(places, turned[i % 2][:, :].rearrange("p (h d) -> p h d", h=HEADS).unsqueeze(2)
                                       .to_broadcast([P, HEADS, 2, D1]), ACT.Copy).then_inc(s["turned_hi"], 1)
                    elif step[0] == "nturn":
                        g = step[1]
                        for j, (bank, ready, _) in enumerate(uses):
                            w, t = j // 2, j % 2
                            act.wait_ge(s["f_ready"], ready)
                            act.activation(stackT[w][:, 4 * g:4 * g + 4, t * P:(t + 1) * P], F_ps[bank][:, :]
                                           .rearrange("p (h q) -> p h q", h=4), ACT.Copy).then_inc(s["f_act"], 1)
                    elif step[0] == "nval":
                        t = step[1]
                        act.wait_ge(s["v_full"], 2 * (b + 1) + t + 1)
                        act.activation(v[t][:, :, 0, :], vfull[:, :].rearrange("p (h d) -> p h d", h=HEADS), ACT.Copy).then_inc(s["v_hi"], 1)
                    elif step[0] == "pot":
                        t = step[1]
                        bank, ready, _ = uses[0]
                        act.wait_ge(s["f_ready"], ready)
                        act.activation(oTh[t][:, :, :], F_ps[bank][:, :], ACT.Copy).then_inc(s["ot_hi"], 1)

            body(-1, FIRST1, spare_first())
            with act.Fori(0, B - 1) as b:
                body(b, ORDER1, spare(b))
            body(B - 1, LAST1, spare(B - 1))
            body(B, FINISH1, spare_last())

        @block.vector
        def _(dve):
            dve.sem_inc(s["turned_lo"], 2)
            dve.sem_inc(s["p_lo"], 2)
            dve.sem_inc(s["o_ready"], 2)

            def own_step(own, last):
                last.then_inc(s["own_dve"], 1)
                stand(dve, s["own_dve"], own.next(), s["stood"])

            def outputs(b, g, own):
                dve.wait_ge(s["pv_done"], NU1 * b + 3 * g + 3 + 2)
                dve.wait_ge(s["o_ready"], 4 * b + g + 2)
                dve.reciprocal(rsum[:, :, :], sums[:, :, 4 * g:4 * g + 4])
                own_step(own, dve.tensor_reduce(osum[:, :, :, :].rearrange("p t h d -> p (t h) d"), O_ps[g % 2][:, :]
                                                .rearrange("p (g e d) -> p g d e", e=2, d=D1), AX.X, ALU.add))
                dve.tensor_tensor(o[:, :, 4 * D1 * g:4 * D1 * (g + 1)].rearrange("p t (h d) -> p t h d", h=4), osum[:, :, :, :],
                                  rsum[:, :, :].unsqueeze(3).to_broadcast([P, T, 4, D1]), ALU.mult).then_inc(s["o_ready"], 1)

            def body(b, order, ring, own):
                u0 = NU1 * b
                for step in order:
                    n, by = spare_uses(step[0])
                    uses = [ring.next(by) for _ in range(n)]
                    if step[0] == "S":
                        u = step[1]
                        t, heads, g = UNITS1[u]
                        dve.wait_ge(s["s_ready"], u0 + u + 1)
                        dve.wait_ge(s["exp_done"], u0 + u + 1)
                        dve.tensor_reduce(negmax[:, u % 2, 0:len(heads)], S_ps[u % 2][:, :]
                                          .rearrange("p (h j) -> p h j", h=len(heads)), AX.X, ALU.max, negate=True).then_inc(s["max_ready"], 1)
                    elif step[0] == "T":
                        u = step[1]
                        dve.wait_ge(s["p_hi"], u0 + u + 1)
                        dve.tensor_tensor(pTl[u % 2][:, :, :], T_ps[u % 2][:, :].rearrange("p (a q) -> p a q", a=4), fp(pTh[u % 2][:, :, :]), ALU.subtract).then_inc(s["p_lo"], 1)
                    elif step[0] == "V":
                        if step[1] % 3 == 2:
                            outputs(b, step[1] // 3, own)
                    elif step[0] == "nstat":
                        dve.wait_ge(s["xs_in"], 16 * (b + 2))
                        for t in range(T):
                            last = dve.bn_stats(bn[:, 0, t, :], xs[:, t, :])
                        own_step(own, last)
                        for t in range(T):
                            last = dve.bn_aggr(mv[:, 0, t, :], bn[:, 0, t, :])
                        last.then_inc(s["stat"], 1)
                    elif step[0] in ("nnorm", "pnorm"):
                        which, rows, n, done = (0, xs, b + 2, "z_ready") if step[0] == "nnorm" else (1, acc, b + 1, "out_ready")
                        stand(dve, s["rstd_ready" if which == 0 else "rstd2_ready"], n, s["stood"])
                        for t in range(T):
                            last = dve.tensor_scalar(rows[:, t, :], rows[:, t, :], mv[:, which, t, 0:1], rstd[:, which, t:t + 1],
                                                     ALU.subtract, ALU.mult)
                        last.then_inc(s[done], 1)
                    elif step[0] == "nz":
                        for j, (bank, _, _) in enumerate(uses):
                            dve.wait_ge(s["z_hi"], 2 * (b + 1) + j + 1)
                            dve.tensor_tensor(zl[:, 2 * j:2 * j + 2, :], F_ps[bank][:, :].rearrange("p (a q) -> p a q", a=2), fp(zh[:, 2 * j:2 * j + 2, :]),
                                              ALU.subtract).then_inc(s["f_dve"], 1)
                    elif step[0] == "nproj":
                        i = step[1]
                        bank, ready, _ = uses[0]
                        dve.wait_ge(s["f_ready"], ready)
                        dve.wait_ge(s["turned_ready"], 4 * (b + 1) + i + 1)
                        dve.tensor_tensor(biased[i % 2][:, :], F_ps[bank][:, :], bias[i % 2][:, :], ALU.add).then_inc(s["f_dve"], 1)
                    elif step[0] == "nstack":
                        turned_lo(b, step[1])
                    elif step[0] == "nval":
                        t = step[1]
                        bank, ready, _ = uses[0]
                        dve.wait_ge(s["f_ready"], ready)
                        dve.wait_ge(s["f_dve"], ring.made["dve"] - 1)
                        dve.tensor_tensor(vfull[:, :], F_ps[bank][:, :], bias[2][:, :], ALU.add).then_inc(s["v_full"], 1)
                        dve.wait_ge(s["v_hi"], 2 * (b + 1) + t + 1)
                        dve.tensor_tensor(v[t][:, :, 1, :], vfull[:, :].rearrange("p (h d) -> p h d", h=HEADS), fp(v[t][:, :, 0, :]),
                                          ALU.subtract).then_inc(s["f_dve"], 1)
                    elif step[0] == "pot":
                        t = step[1]
                        bank, _, _ = uses[0]
                        dve.wait_ge(s["ot_hi"], 2 * b + t + 1)
                        dve.tensor_tensor(oTl[t][:, :, :], F_ps[bank][:, :].rearrange("p (a q) -> p a q", a=KT), fp(oTh[t][:, :, :]), ALU.subtract).then_inc(s["f_dve"], 1)
                    elif step[0] == "py":
                        t = step[1]
                        bank, ready, _ = uses[0]
                        dve.wait_ge(s["base_ready"], b + 1)
                        dve.wait_ge(s["f_ready"], ready)
                        dve.scalar_tensor_tensor(acc[:, t, :], acc[:, t, :], 2.0, F_ps[bank][:, :], ALU.mult, ALU.add).then_inc(s["f_dve"], 1)
                        if t == T - 1:
                            dve.wait_ge(s["f_dve"], ring.made["dve"])
                            for t in range(T):
                                last = dve.bn_stats(bn[:, 1, t, :], acc[:, t, :])
                            own_step(own, last)
                            for t in range(T):
                                last = dve.bn_aggr(mv[:, 1, t, :], bn[:, 1, t, :])
                            last.then_inc(s["stat2"], 1)

            def turned_lo(b, i):
                w, t = i % 2, i // 2
                dve.wait_ge(s["turned_hi"], 4 * (b + 1) + i + 1)
                a = 2 if w == 0 else 1
                dve.tensor_tensor(stack[w][t][:, :, a, :], turned[i % 2][:, :].rearrange("p (h d) -> p h d", h=HEADS),
                                  fp(stack[w][t][:, :, 0, :]), ALU.subtract).then_inc(s["turned_lo"], 1)

            body(-1, FIRST1, spare_first(), OwnSteps())
            per_body = 1 + 4 + 1
            with dve.Fori(0, B - 1) as b:
                body(b, ORDER1, spare(b), OwnSteps(1 + per_body * b))
            body(B - 1, LAST1, spare(B - 1), OwnSteps(1 + per_body * (B - 1)))
            body(B, FINISH1, spare_last(), OwnSteps(1 + per_body * (B - 1) + 5))

        @block.tensor
        def _(pe):
            pe.sem_inc(s["t_ready"], 2)
            pe.sem_inc(s["pv_done"], 2)

            def body(b, order, ring, first):
                u0 = NU1 * b
                split = {}
                if not first and ("S", 0) in order:
                    pe.wait_ge(s["f_act"], 16 + 16 * b)
                    pe.wait_ge(s["f_dve"], 8 + 12 * b)
                for step in order:
                    n, by = spare_uses(step[0])
                    uses = [ring.next(by) for _ in range(n)]
                    if step[0] == "S":
                        u = step[1]
                        t, heads, g = UNITS1[u]
                        nj = P * (t + 1)
                        pe.wait_ge(s["exp_done"], u0 + u + 1)
                        for j, h in enumerate(heads):
                            pe.matmul(S_ps[u % 2][:, j * nj:(j + 1) * nj], stackT[0][:, h, t * P:(t + 1) * P],
                                      stackT[1][:, h, 0:nj], start=True, stop=False)
                            last = pe.matmul(S_ps[u % 2][:, (j + 1) * nj - P:(j + 1) * nj], identb[:, :], causal[:, :],
                                             start=False, stop=True)
                        last.then_inc(s["s_ready"], 1)
                    elif step[0] == "T":
                        u = step[1]
                        pe.wait_ge(s["exp_done"], u0 + u + 3)
                        pe.wait_ge(s["p_lo"], u0 + u + 1)
                        for a in range(4):
                            last = pe.transpose(T_ps[u % 2][:, a * P:(a + 1) * P], probs[u % 2][:, a * P:(a + 1) * P], ident[:, :])
                        last.then_inc(s["t_ready"], 1)
                    elif step[0] == "V":
                        u = step[1]
                        t, heads, g = UNITS1[u]
                        pe.wait_ge(s["p_lo"], u0 + u + 3)
                        if u % 3 == 0:
                            pe.wait_ge(s["o_ready"], 4 * b + g + 1)
                        for j, h in enumerate(heads):
                            to = O_ps[g % 2][:, (t * 4 + h % 4) * 2 * D1:(t * 4 + h % 4 + 1) * 2 * D1]
                            for a in range(t + 1):
                                pe.matmul(to, pTh[u % 2][:, j * (t + 1) + a, :], v[a][:, h, :, :], start=a == 0, stop=False)
                                last = pe.matmul(to[:, 0:D1], pTl[u % 2][:, j * (t + 1) + a, :], v[a][:, h, 0, :],
                                                 start=False, stop=a == t)
                        last.then_inc(s["pv_done"], 1)
                    elif step[0] == "nz":
                        pe.wait_ge(s["z_ready"], b + 2)
                        for j, (bank, _, before) in enumerate(uses):
                            wait_spare(pe, before, first)
                            for a in range(2):
                                for t in range(T):
                                    k = 2 * j + a
                                    last = pe.transpose(F_ps[bank][:, a * L + t * P:a * L + (t + 1) * P],
                                                        xs[:, t, k * P:(k + 1) * P], ident[:, :])
                            last.then_inc(s["f_ready"], 1)
                    elif step[0] == "nproj" or step[0] == "nval":
                        i = step[1]
                        w, t = (i % 2, i // 2) if step[0] == "nproj" else (2, i)
                        bank, _, before = uses[0]
                        wait_spare(pe, before, first)
                        if step == ("nproj", 0):
                            pe.wait_ge(s["f_dve"], ring.made["dve"] - 1)
                        for k in range(KT):
                            last = product3(pe, F_ps[bank][:, :], (zh[:, k, t * P:(t + 1) * P], zl[:, k, t * P:(t + 1) * P]),
                                            (wh[w][:, k, :], wl[w][:, k, :]), k == 0, k == KT - 1)
                        last.then_inc(s["f_ready"], 1)
                    elif step[0] == "nturn":
                        g = step[1]
                        if g == 0:
                            pe.wait_ge(s["stacked"], 4 * (b + 2))
                        for j, (bank, _, before) in enumerate(uses):
                            w, t = j // 2, j % 2
                            wait_spare(pe, before, first)
                            for a in range(4):
                                last = pe.transpose(F_ps[bank][:, a * P:(a + 1) * P], fp(stack[w][t][:, 4 * g + a, :, :]), ident[:, :])
                            last.then_inc(s["f_ready"], 1)
                    elif step[0] == "pot":
                        t = step[1]
                        bank, _, before = uses[0]
                        split[t] = ring.made["dve"]
                        wait_spare(pe, before, first)
                        pe.wait_ge(s["o_ready"], 4 * b + 2)
                        for k in range(KT):
                            last = pe.transpose(F_ps[bank][:, k * P:(k + 1) * P], o[:, t, k * P:(k + 1) * P], ident[:, :])
                        last.then_inc(s["f_ready"], 1)
                    elif step[0] == "py":
                        t = step[1]
                        bank, _, before = uses[0]
                        wait_spare(pe, before, first)
                        pe.wait_ge(s["f_dve"], split[t])
                        for k in range(KT):
                            last = product3(pe, F_ps[bank][:, :], (oTh[t][:, k, :], oTl[t][:, k, :]),
                                            (wh[3][:, k, :], wl[3][:, k, :]), k == 0, k == KT - 1)
                        last.then_inc(s["f_ready"], 1)

            body(-1, FIRST1, spare_first(), True)
            with pe.Fori(0, B - 1) as b:
                body(b, ORDER1, spare(b), False)
            body(B - 1, LAST1, spare(B - 1), False)
            body(B, FINISH1, spare_last(), False)



D2 = 64
EMBED = HEADS * D2
PAIRS = HEADS // 2
WINDOW = 128

ORDER2 = []
for _m in range(PAIRS):
    ORDER2 += [("S", 2 * _m), ("T", 2 * _m - 1), ("prj", _m + 1), ("V", 2 * _m - 2), ("ot", _m - 2),
               ("S", 2 * _m + 1), ("T", 2 * _m), ("V", 2 * _m - 1), ("y", _m - 2)]
    if _m == 1:
        ORDER2 += [("xt", 0)]
    if _m == 0:
        ORDER2 += [("norm", 0)]
ORDER2 = [st for st in ORDER2 if st[1] >= 0 and st != ("prj", PAIRS)]
ORDER2 += [("T", 15), ("nx", 0), ("V", 14), ("ot", 6), ("V", 15), ("y", 6), ("nv", 0), ("ot", 7), ("nprj", 0),
           ("nv", 1), ("y", 7), ("nv", 2), ("nv", 3)]
FIRST2 = [("nx", 0), ("nprj", 0), ("nv", 0), ("nv", 1), ("nv", 2), ("nv", 3)]
LAST2 = [st for st in ORDER2 if st[0] not in ("nx", "nprj", "nv")] + [("norm", 1), ("xt", 1)]


def cross_attention(nc, x1, context, weights, x2, x2T, pooled_out):
    with ExitStack() as ctx:
        def sb(name, shape, dt=F32):
            return ctx.enter_context(nc.sbuf_tensor(name, shape, dt))

        def sem(name):
            return ctx.enter_context(nc.semaphore(name))

        def banks(name, n):
            return [ctx.enter_context(nc.psum_tensor(f"{name}{i}", [P, 512], F32)) for i in range(n)]

        rows = [KT, KT, KT, PAIRS]
        cols = [EMBED, EMBED, EMBED, D]
        wh = [sb(f"c_wh{i}", [P, rows[i], cols[i]], F32R) for i in range(4)]
        wl = [sb(f"c_wl{i}", [P, rows[i], cols[i]], F32R) for i in range(4)]
        ident = sb("c_ident", [P, P])
        identb = sb("c_identb", [P, P], BF16)
        far = [sb(f"c_far{t}", [P, P], BF16) for t in range(T)]
        half = sb("c_half", [P, T])
        pooled = sb("c_pooled", [P, KT, B + 1])
        qh = [sb(f"c_qh{i}", [P, 2, L], F32R) for i in range(2)]
        ql = [sb(f"c_ql{i}", [P, 2, L], F32R) for i in range(2)]
        kh = [sb(f"c_kh{i}", [P, L], F32R) for i in range(2)]
        kl = [sb(f"c_kl{i}", [P, L], F32R) for i in range(2)]
        acc = sb("c_acc", [P, T, D])
        mv = sb("c_mv", [P, T, 2])
        rstd = sb("c_rstd", [P, T])

        S_ps, T_ps, F_ps, O_ps, Y_ps = banks("c_S", 2), banks("c_T", 2), banks("c_F", 1)[0], banks("c_O", 1)[0], banks("c_Y", 2)

        with ExitStack() as sctx:
            stage = [sctx.enter_context(nc.sbuf_tensor(f"c_raw{i}", [P, KT * EMBED], F32)) for i in range(3)]
            raw = [stage[i % 3][:, :].rearrange("p (t n) -> p t n", t=rows[i]) for i in range(4)]
            w_in = [sctx.enter_context(nc.semaphore(f"c_w_in{i}")) for i in range(4)]
            made = sctx.enter_context(nc.semaphore("c_made"))
            w_hi = sctx.enter_context(nc.semaphore("c_w_hi"))
            w_lo = sctx.enter_context(nc.semaphore("c_w_lo"))
            block = sctx.enter_context(nc.Block())

            @block.sync
            def _(sp):
                for i in range(4):
                    if i == 3:
                        sp.wait_ge(w_lo, 1)
                    sp.dma_start(raw[i], weights[i].rearrange("(t p) n -> p t n", p=P)).then_inc(w_in[i], 16)

            @block.gpsimd
            def _(pool):
                for m in (ident, identb, far[0], far[1]):
                    last = pool.memset(m[:, :], 0.0)
                last.then_inc(made, 1)
                pool.memset(half[:, :], -0.5)
                for m in (acc[:, :, :], mv[:, :, :], rstd[:, :]):
                    pool.memset(m, 0.0)
                for i in range(2):
                    pool.memset(fp(qh[i][:, :, :]), 0.0)
                    pool.memset(fp(ql[i][:, :, :]), 0.0)
                pool.wait_ge(made, 1)
                for m in (ident, identb):
                    pool.affine_select(m[:, :], m[:, :], [[-1, P]], ALU.not_equal, 1.0, base=0, channel_multiplier=1)
                pool.affine_select(far[0][:, :], far[0][:, :], [[-1, P]], ALU.is_ge, MASKED, base=0, channel_multiplier=1)
                pool.affine_select(far[1][:, :], far[1][:, :], [[1, P]], ALU.is_ge, MASKED, base=0, channel_multiplier=-1)

            @block.vector
            def _(dve):
                for i in range(4):
                    dve.wait_ge(w_in[i], 16)
                    dve.wait_ge(w_hi, i + 1)
                    dve.tensor_tensor(wl[i][:, :, :], raw[i], fp(wh[i][:, :, :]), ALU.subtract).then_inc(w_lo, 1)

            @block.scalar
            def _(act):
                for i in range(4):
                    act.wait_ge(w_in[i], 16)
                    act.activation(wh[i][:, :, :], raw[i], ACT.Copy).then_inc(w_hi, 1)

        xs = sb("c_xs", [P, 2, T, D])
        inTh = sb("c_inTh", [P, 2, KT, L], F32R)
        inTl = sb("c_inTl", [P, 2, KT, L], F32R)
        v = [sb(f"c_v{t}", [P, HEADS, 2, D2], F32R) for t in range(T)]
        negmax = sb("c_negmax", [P, 2, 2])
        probs = [sb(f"c_probs{i}", [P, 2, L]) for i in range(2)]
        sums = sb("c_sums", [P, T, HEADS])
        pTh = [sb(f"c_pTh{i}", [P, 4, P], F32R) for i in range(2)]
        pTl = [sb(f"c_pTl{i}", [P, 4, P], F32R) for i in range(2)]
        rsum = sb("c_rsum", [P, T, 2])
        o = sb("c_o", [P, T, 2, D2])
        oTh = [sb(f"c_oTh{i}", [P, L], F32R) for i in range(2)]
        oTl = [sb(f"c_oTl{i}", [P, L], F32R) for i in range(2)]
        outT = sb("c_outT", [P, KT, L])
        bn = sb("c_bn", [P, T, 6])
        ve = sb("c_ve", [P, T])

        names = ["xs_in", "acc_in", "out_done", "outT_done", "pooled_done", "s_ready", "s_dve", "exp_done", "max_ready", "n_hi",
                 "t_ready", "t_hi", "t_dve", "f_ready", "f_hi", "f_dve", "pv_done", "o_ready", "y_ready", "y_dve",
                 "stat", "rstd_ready", "out_ready", "outT_ready", "own_dve", "own_pool", "stood"]
        s = {n: sem("c_" + n) for n in names}
        block = ctx.enter_context(nc.Block())

        def score_banks(b):
            return SpareBanks(8 + 26 * b, 8 + 10 * b, 2 + 16 * b)

        def turn_banks(b):
            return SpareBanks(24 * b, 24 * b + 2, 0)

        def score_uses(kind):
            return {"S": (1, "act"), "xt": (2, "dve"), "nx": (4, "dve"), "nv": (1, "dve")}.get(kind, (0, "dve"))

        def turn_uses(kind):
            return 1 if kind in ("T", "ot") else 0

        def project_count(b, kind, m):
            return PAIRS * (b + (kind == "nprj")) + m + 1

        def rows_of(tensor, b):
            return tensor[b].rearrange("(t p) d -> p t d", p=P)

        @block.sync
        def _(sp):
            sp.sem_inc(s["outT_done"], 16)

            def load_inputs(b, transposed):
                if transposed is not None:
                    sp.wait_ge(s["s_ready"], transposed)
                sp.dma_start(xs[:, 0, :, :], rows_of(x1, b + 1)).then_inc(s["xs_in"], 16)
                sp.dma_start(xs[:, 1, :, :], rows_of(context, b)).then_inc(s["xs_in"], 16)

            def batch(b, more):
                if more:
                    load_inputs(b + 1, 4 if isinstance(b, int) else 8 + 26 * b - 4)
                store(b - 1)
                store_transposed(b)
                sp.wait_ge(s["out_done"], 16 * (b + 1))
                sp.dma_start(acc[:, :, :], rows_of(x1, b + 1)).then_inc(s["acc_in"], 16)

            def store(b):
                sp.wait_ge(s["out_ready"], b + 2)
                sp.dma_start(rows_of(x2, b + 1), acc[:, :, :]).then_inc(s["out_done"], 16)

            def store_transposed(b):
                sp.wait_ge(s["outT_ready"], 2 * b + 2)
                sp.dma_start(x2T[b], outT[:, :, :]).then_inc(s["outT_done"], 16)

            load_inputs(0, None)
            batch(0, True)
            with sp.Fori(1, B - 1) as b:
                batch(b, True)
            batch(B - 1, False)
            store(B - 1)
            store_transposed(B)
            sp.wait_ge(s["s_dve"], 8 + 10 * (B - 1) + 4)
            sp.dma_start(pooled_out, pooled[:, :, :]).then_inc(s["pooled_done"], 16)
            sp.wait_ge(s["pooled_done"], 16)
            sp.wait_ge(s["out_done"], 16 * (B + 1))
            sp.wait_ge(s["outT_done"], 16 * (B + 2))

        @block.gpsimd
        def _(pool):
            pool.sem_inc(s["rstd_ready"], 1)
            with pool.Fori(0, B) as b:
                stand(pool, s["stat"], b + 1, s["stood"])
                pool.tensor_scalar(ve[:, :], mv[:, :, 1], EPS, None, ALU.add).then_inc(s["own_pool"], 1)
                pool.wait_ge(s["own_pool"], b + 1)
                pool.tensor_tensor(rstd[:, :], ve[:, :], half[:, :], ALU.pow).then_inc(s["rstd_ready"], 1)

        @block.scalar
        def _(act):
            act.sem_inc(s["exp_done"], 2)

            def body(b, order, ring, turns):
                for kind, i in order:
                    n, by = score_uses(kind)
                    uses = [ring.next(by) for _ in range(n)]
                    uses += [turns.next("dve") for _ in range(turn_uses(kind))]
                    if kind == "S":
                        act.wait_ge(s["max_ready"], 16 * b + i + 1)
                        for j in range(2):
                            last = act.activation(probs[i % 2][:, j, :], S_ps[uses[0][0]][:, j * L:(j + 1) * L], ACT.Exp,
                                                  bias=negmax[:, i % 2, j:j + 1], accum_out=sums[:, i % 2, i - i % 2 + j:i - i % 2 + j + 1])
                        last.then_inc(s["exp_done"], 1)
                    elif kind in ("T", "ot"):
                        bank, ready, _ = uses[0]
                        act.wait_ge(s["t_ready"], ready)
                        to, n = (pTh[i % 2][:, :, :], 512) if kind == "T" else (oTh[i % 2][:, :], L)
                        act.activation(to, T_ps[bank][:, 0:n], ACT.Copy).then_inc(s["t_hi"], 1)
                    elif kind in ("prj", "nprj"):
                        act.wait_ge(s["f_ready"], project_count(b, kind, i))
                        for j in range(2):
                            h = slice(j * D2, (j + 1) * D2)
                            act.activation(qh[i % 2][h, j, :], F_ps[h, 0:L], ACT.Copy, scale=D2 ** -0.5)
                        act.activation(kh[i % 2][:, :], F_ps[:, L:2 * L], ACT.Copy).then_inc(s["f_hi"], 1)
                    elif kind == "nx":
                        for j, (bank, ready, _) in enumerate(uses):
                            act.wait_ge(s["s_ready"], ready)
                            act.activation(inTh[:, j // 2, 2 * (j % 2):2 * (j % 2) + 2, :], S_ps[bank][:, :], ACT.Copy).then_inc(s["n_hi"], 1)
                    elif kind == "nv":
                        bank, ready, _ = uses[0]
                        act.wait_ge(s["s_ready"], ready)
                        act.activation(v[i // 2][:, 8 * (i % 2):8 * (i % 2) + 8, 0, :], S_ps[bank][:, :]
                                       .rearrange("p (h d) -> p h d", h=8), ACT.Copy).then_inc(s["n_hi"], 1)
                    elif kind == "xt":
                        act.wait_ge(s["outT_done"], 16 * (b + i + 1))
                        for j, (bank, ready, _) in enumerate(uses):
                            act.wait_ge(s["s_ready"], ready)
                            act.activation(outT[:, 2 * j:2 * j + 2, :], S_ps[bank][:, :], ACT.Copy).then_inc(s["outT_ready"], 1)

            body(-1, FIRST2, SpareBanks(0, 0, 0), turn_banks(0))
            with act.Fori(0, B - 1) as b:
                body(b, ORDER2, score_banks(b), turn_banks(b))
            body(B - 1, LAST2, score_banks(B - 1), turn_banks(B - 1))

        @block.vector
        def _(dve):
            dve.sem_inc(s["t_dve"], 2)
            dve.sem_inc(s["f_dve"], 1)
            dve.sem_inc(s["o_ready"], 1)
            dve.sem_inc(s["y_dve"], 1)

            def outputs(b, m, own):
                dve.wait_ge(s["pv_done"], PAIRS * b + m + 1)
                dve.wait_ge(s["o_ready"], PAIRS * b + m + 1)
                dve.reciprocal(rsum[:, :, :], sums[:, :, 2 * m:2 * m + 2])
                dve.tensor_reduce(o[:, :, :, :].rearrange("p t h d -> p (t h) d"), O_ps[:, :]
                                  .rearrange("p (g e d) -> p g d e", e=2, d=D2), AX.X, ALU.add).then_inc(s["own_dve"], 1)
                stand(dve, s["own_dve"], own.next(), s["stood"])
                dve.tensor_tensor(o[:, :, :, :], o[:, :, :, :], rsum[:, :, :].unsqueeze(3).to_broadcast([P, T, 2, D2]),
                                  ALU.mult).then_inc(s["o_ready"], 1)

            def body(b, order, ring, turns, own):
                for kind, i in order:
                    n, by = score_uses(kind)
                    uses = [ring.next(by) for _ in range(n)]
                    uses += [turns.next("dve") for _ in range(turn_uses(kind))]
                    if kind == "S":
                        bank, ready, _ = uses[0]
                        dve.wait_ge(s["s_ready"], ready)
                        dve.wait_ge(s["exp_done"], 16 * b + i + 1)
                        dve.tensor_reduce(negmax[:, i % 2, :], S_ps[bank][:, :].rearrange("p (h j) -> p h j", h=2),
                                          AX.X, ALU.max, negate=True).then_inc(s["max_ready"], 1)
                    elif kind in ("T", "ot"):
                        bank, ready, _ = uses[0]
                        dve.wait_ge(s["t_hi"], ready)
                        if kind == "T":
                            dve.tensor_tensor(pTl[i % 2][:, :, :], T_ps[bank][:, :].rearrange("p (a q) -> p a q", a=4),
                                              fp(pTh[i % 2][:, :, :]), ALU.subtract).then_inc(s["t_dve"], 1)
                        else:
                            dve.tensor_tensor(oTl[i % 2][:, :], T_ps[bank][:, 0:L], fp(oTh[i % 2][:, :]), ALU.subtract).then_inc(s["t_dve"], 1)
                    elif kind == "V":
                        if i % 2 == 1:
                            outputs(b, i // 2, own)
                    elif kind in ("prj", "nprj"):
                        dve.wait_ge(s["f_hi"], project_count(b, kind, i))
                        for j in range(2):
                            h = slice(j * D2, (j + 1) * D2)
                            dve.scalar_tensor_tensor(ql[i % 2][h, j, :], F_ps[h, 0:L], D2 ** -0.5, fp(qh[i % 2][h, j, :]),
                                                     ALU.mult, ALU.subtract)
                        dve.tensor_tensor(kl[i % 2][:, :], F_ps[:, L:2 * L], fp(kh[i % 2][:, :]), ALU.subtract).then_inc(s["f_dve"], 1)
                    elif kind == "nx":
                        for j, (bank, _, _) in enumerate(uses):
                            dve.wait_ge(s["n_hi"], 8 * (b + 1) + j + 1)
                            at = inTh[:, j // 2, 2 * (j % 2):2 * (j % 2) + 2, :]
                            dve.tensor_tensor(inTl[:, j // 2, 2 * (j % 2):2 * (j % 2) + 2, :], S_ps[bank][:, :]
                                              .rearrange("p (a q) -> p a q", a=2), fp(at), ALU.subtract).then_inc(s["s_dve"], 1)
                    elif kind == "nv":
                        bank, _, _ = uses[0]
                        dve.wait_ge(s["n_hi"], 8 * (b + 1) + 4 + i + 1)
                        h = slice(8 * (i % 2), 8 * (i % 2) + 8)
                        dve.tensor_tensor(v[i // 2][:, h, 1, :], S_ps[bank][:, :].rearrange("p (h d) -> p h d", h=8),
                                          fp(v[i // 2][:, h, 0, :]), ALU.subtract).then_inc(s["s_dve"], 1)
                    elif kind == "xt":
                        for j, (bank, _, _) in enumerate(uses):
                            dve.wait_ge(s["outT_ready"], 2 * (b + i) + j + 1)
                            dve.tensor_reduce(pooled[:, 2 * j:2 * j + 2, b + i], S_ps[bank][:, :].rearrange("p (a q) -> p a q", a=2),
                                              AX.X, ALU.add).then_inc(s["s_dve"], 1)
                    elif kind == "norm":
                        stand(dve, s["rstd_ready"], b + i + 1, s["stood"])
                        for t in range(T):
                            last = dve.tensor_scalar(acc[:, t, :], acc[:, t, :], mv[:, t, 0:1], rstd[:, t:t + 1], ALU.subtract, ALU.mult)
                        last.then_inc(s["out_ready"], 1)
                    elif (kind, i) == ("y", PAIRS - 1):
                        dve.wait_ge(s["acc_in"], 16 * (b + 1))
                        dve.wait_ge(s["y_ready"], b + 1)
                        for t in range(T):
                            last = dve.tensor_tensor(acc[:, t, :], Y_ps[t][:, :], acc[:, t, :], ALU.add)
                        last.then_inc(s["y_dve"], 1)
                        dve.wait_ge(s["y_dve"], b + 2)
                        for t in range(T):
                            last = dve.bn_stats(bn[:, t, :], acc[:, t, :])
                        last.then_inc(s["own_dve"], 1)
                        stand(dve, s["own_dve"], own.next(), s["stood"])
                        for t in range(T):
                            last = dve.bn_aggr(mv[:, t, :], bn[:, t, :])
                        last.then_inc(s["stat"], 1)

            body(-1, FIRST2, SpareBanks(0, 0, 0), turn_banks(0), OwnSteps())
            per_body = PAIRS + 1
            with dve.Fori(0, B - 1) as b:
                body(b, ORDER2, score_banks(b), turn_banks(b), OwnSteps(per_body * b))
            body(B - 1, LAST2, score_banks(B - 1), turn_banks(B - 1), OwnSteps(per_body * (B - 1)))

        @block.tensor
        def _(pe):
            def wait_score_bank(before, first):
                by, count = before
                if not (first and count <= 0):
                    pe.wait_ge(s["exp_done" if by == "act" else "s_dve"], count)

            def body(b, order, ring, turns, first):
                turned = {}
                if not first:
                    pe.wait_ge(s["s_dve"], 8 + 10 * b)
                for kind, i in order:
                    n, by = score_uses(kind)
                    uses = [ring.next(by) for _ in range(n)]
                    if turn_uses(kind):
                        bank, ready, before = turns.next("dve")
                        turned[kind, i] = turns.made["dve"]
                        pe.wait_ge(s["t_dve"], before[1])
                    if kind == "S":
                        bank, _, before = uses[0]
                        t, m = i % 2, i // 2
                        wait_score_bank(before, first)
                        if t == 0:
                            pe.wait_ge(s["f_dve"], project_count(b, kind, m) + 1)
                        q = slice(t * P, (t + 1) * P)
                        for j in range(2):
                            out = S_ps[bank][:, j * L:(j + 1) * L]
                            product3(pe, out, (qh[m % 2][:, j, q], ql[m % 2][:, j, q]), (kh[m % 2][:, :], kl[m % 2][:, :]), True, False)
                            last = pe.matmul(out[:, (1 - t) * P:(2 - t) * P], identb[:, :], far[t][:, :], start=False, stop=True)
                        last.then_inc(s["s_ready"], 1)
                    elif kind == "T":
                        pe.wait_ge(s["exp_done"], 16 * b + i + 3)
                        for a in range(4):
                            last = pe.transpose(T_ps[bank][:, a * P:(a + 1) * P], probs[i % 2][:, a // 2, (a % 2) * P:(a % 2 + 1) * P], ident[:, :])
                        last.then_inc(s["t_ready"], 1)
                    elif kind == "V":
                        t, m = i % 2, i // 2
                        pe.wait_ge(s["t_dve"], turned["T", i])
                        if t == 0:
                            pe.wait_ge(s["o_ready"], PAIRS * b + m + 1)
                        for j in range(2):
                            to = O_ps[:, (t * 2 + j) * 2 * D2:(t * 2 + j + 1) * 2 * D2]
                            for a in range(T):
                                pe.matmul(to, pTh[i % 2][:, j * 2 + a, :], v[a][:, 2 * m + j, :, :], start=a == 0, stop=False)
                                last = pe.matmul(to[:, 0:D2], pTl[i % 2][:, j * 2 + a, :], v[a][:, 2 * m + j, 0, :], start=False, stop=a == 1)
                        if t == 1:
                            last.then_inc(s["pv_done"], 1)
                    elif kind in ("prj", "nprj"):
                        if kind == "nprj":
                            pe.wait_ge(s["s_dve"], ring.made["dve"] - (0 if first else 1))
                        pe.wait_ge(s["f_dve"], project_count(b, kind, i))
                        for w in range(2):
                            for k in range(KT):
                                last = product3(pe, F_ps[:, w * L:(w + 1) * L], (wh[w][:, k, i * P:(i + 1) * P], wl[w][:, k, i * P:(i + 1) * P]),
                                                (inTh[:, w, k, :], inTl[:, w, k, :]), k == 0, k == KT - 1)
                        last.then_inc(s["f_ready"], 1)
                    elif kind == "ot":
                        pe.wait_ge(s["o_ready"], PAIRS * b + i + 2)
                        for t in range(T):
                            last = pe.transpose(T_ps[bank][:, t * P:(t + 1) * P], o[:, t, :, :], ident[:, :])
                        last.then_inc(s["t_ready"], 1)
                    elif kind == "y":
                        pe.wait_ge(s["t_dve"], turned["ot", i])
                        if i == 0:
                            pe.wait_ge(s["y_dve"], b + 1)
                        for t in range(T):
                            q = slice(t * P, (t + 1) * P)
                            last = product3(pe, Y_ps[t][:, :], (oTh[i % 2][:, q], oTl[i % 2][:, q]), (wh[3][:, i, :], wl[3][:, i, :]),
                                            i == 0, i == PAIRS - 1)
                        if i == PAIRS - 1:
                            last.then_inc(s["y_ready"], 1)
                    elif kind == "nx":
                        pe.wait_ge(s["xs_in"], 32 * (b + 2))
                        for j, (bank, _, before) in enumerate(uses):
                            wait_score_bank(before, first)
                            for a in range(2):
                                for t in range(T):
                                    k = 2 * (j % 2) + a
                                    last = pe.transpose(S_ps[bank][:, a * L + t * P:a * L + (t + 1) * P], xs[:, j // 2, t, k * P:(k + 1) * P], ident[:, :])
                            last.then_inc(s["s_ready"], 1)
                    elif kind == "nv":
                        bank, _, before = uses[0]
                        wait_score_bank(before, first)
                        t, c = i // 2, slice((i % 2) * 512, (i % 2 + 1) * 512)
                        if i == 0:
                            pe.wait_ge(s["s_dve"], ring.made["dve"] - 1)
                        for k in range(KT):
                            last = product3(pe, S_ps[bank][:, :], (inTh[:, 1, k, t * P:(t + 1) * P], inTl[:, 1, k, t * P:(t + 1) * P]),
                                            (wh[2][:, k, c], wl[2][:, k, c]), k == 0, k == KT - 1)
                        last.then_inc(s["s_ready"], 1)
                    elif kind == "xt":
                        pe.wait_ge(s["out_ready"], b + i + 1)
                        for j, (bank, _, before) in enumerate(uses):
                            wait_score_bank(before, first)
                            for a in range(2):
                                for t in range(T):
                                    k = 2 * j + a
                                    last = pe.transpose(S_ps[bank][:, a * L + t * P:a * L + (t + 1) * P], acc[:, t, k * P:(k + 1) * P], ident[:, :])
                            last.then_inc(s["s_ready"], 1)

            body(-1, FIRST2, SpareBanks(0, 0, 0), turn_banks(0), True)
            with pe.Fori(0, B - 1) as b:
                body(b, ORDER2, score_banks(b), turn_banks(b), False)
            body(B - 1, LAST2, score_banks(B - 1), turn_banks(B - 1), False)



FC = 4
FT = FF // P // FC
RING = 4

CHUNKS = [("w1", 0), ("w1", 1), ("w2", 0), ("w1", 2), ("w2", 1), ("w1", 3), ("w2", 2), ("w2", 3)]
ORDER3 = [("split", ("w2", 3)), ("h", 1), ("nsplit", ("w1", 0)), ("nsplit", ("w1", 1)), ("y", 0), ("nsplit", ("w2", 0)),
          ("h", 2), ("nsplit", ("w1", 2)), ("base", 0), ("y", 1), ("nsplit", ("w2", 1)), ("h", 3), ("nsplit", ("w1", 3)),
          ("nx", 0), ("y", 2), ("nsplit", ("w2", 2)), ("nh", 0), ("y", 3), ("end", 0)]
FIRST3 = [("nx", 0)] + [("nsplit", c) for c in CHUNKS[:2]] + [("nh", 0)] + [("nsplit", c) for c in CHUNKS[2:-1]]
LAST3 = [st for st in ORDER3 if st[0][0] != "n"]


def route(nc, pooled_in, wr, banks, table, etab, btab):
    with ExitStack() as ctx:
        def sb(name, shape, dt=F32):
            return ctx.enter_context(nc.sbuf_tensor("r_" + name, shape, dt))

        pooled = sb("pooled", [P, KT, B + 1])
        wrs = sb("wr", [P, KT, E])
        logits, top = sb("logits", [B, E]), sb("top", [B, 8])
        index = sb("index", [B, 8], mybir.dt.uint32)
        gap, second, total = sb("gap", [B, 1]), sb("second", [B, 1]), sb("total", [B, 1])
        iota_k, iota_s, iota_b = sb("iota_k", [B, 2], I32), sb("iota_s", [B, SLOTS], I32), sb("iota_b", [B, 1], I32)
        pair_no, slot_no = sb("pair_no", [B, 2]), sb("slot_no", [B, SLOTS])
        value = sb("value", [B, 2, 3])
        key = sb("key", [B, 2])
        ident, ones = sb("ident", [B, B]), sb("ones", [B, B])
        spread = sb("spread", [B, B, 2])
        less = sb("less", [B, 2, SLOTS])
        rank = sb("rank", [B, 2])
        chosen = sb("chosen", [B, 2, SLOTS])
        wide = sb("wide", [B, 2, 3, P])
        ps, pk, pt = banks[0:3]
        s = {n: ctx.enter_context(nc.semaphore("r_" + n)) for n in
             ["loaded", "made", "logits_ready", "gap_ready", "second_ready", "spread_ready", "keys_ready", "wide_ready", "table_ready", "own"]}
        block = ctx.enter_context(nc.Block())

        @block.sync
        def _(sp):
            sp.dma_start(pooled[:, :, :], pooled_in).then_inc(s["loaded"], 16)
            sp.dma_start(wrs[:, :, :], wr.rearrange("(t p) e -> p t e", p=P)).then_inc(s["loaded"], 16)

        @block.gpsimd
        def _(pool):
            pool.memset(ident[:, :], 0.0).then_inc(s["made"], 1)
            pool.memset(ones[:, :], 1.0)
            pool.iota(iota_k[:, :], [[1, 2]], base=0, channel_multiplier=2)
            pool.iota(iota_s[:, :], [[1, SLOTS]], base=0, channel_multiplier=0)
            pool.iota(iota_b[:, :], [[1, 1]], base=0, channel_multiplier=1)
            pool.wait_ge(s["made"], 1)
            pool.affine_select(ident[:, :], ident[:, :], [[-1, B]], ALU.not_equal, 1.0, base=0, channel_multiplier=1).then_inc(s["made"], 1)

        @block.scalar
        def _(act):
            act.wait_ge(s["gap_ready"], 1)
            act.activation(second[:, :], gap[:, :], ACT.Exp).then_inc(s["second_ready"], 1)

        @block.tensor
        def _(pe):
            pe.wait_ge(s["loaded"], 32)
            for k in range(KT):
                last = pe.matmul(ps[0:B, 0:E], pooled[:, k, 1:B + 1], wrs[:, k, :], start=k == 0, stop=k == KT - 1)
            last.then_inc(s["logits_ready"], 1)
            pe.wait_ge(s["spread_ready"], 1)
            pe.matmul(pk[0:B, 0:SLOTS], ones[:, :], spread[:, :, :], start=True, stop=True).then_inc(s["keys_ready"], 1)
            pe.wait_ge(s["wide_ready"], 1)
            for c in range(3):
                for k in range(2):
                    last = pe.matmul(pt[:, c * SLOTS:(c + 1) * SLOTS], wide[:, k, c, :], chosen[:, k, :], start=k == 0, stop=k == 1)
            last.then_inc(s["table_ready"], 1)

        @block.vector
        def _(dve):
            done = [0]

            def own(instruction):
                done[0] += 1
                instruction.then_inc(s["own"], 1)
                dve.wait_ge(s["own"], done[0])

            dve.wait_ge(s["made"], 2)
            dve.tensor_copy(pair_no[:, :], iota_k[:, :])
            dve.tensor_copy(slot_no[:, :], iota_s[:, :])
            dve.tensor_copy(value[:, :, 1], iota_b[:, :].to_broadcast([B, 2]))
            dve.wait_ge(s["logits_ready"], 1)
            own(dve.tensor_scalar(logits[:, :], ps[0:B, 0:E], 1.0 / L, None, ALU.mult))
            own(dve.max(top[:, :], logits[:, :]))
            dve.max_index(index[:, :], top[:, :], logits[:, :])
            dve.tensor_tensor(gap[:, :], top[:, 1:2], top[:, 0:1], ALU.subtract).then_inc(s["gap_ready"], 1)
            dve.wait_ge(s["gap_ready"], 1)
            own(dve.tensor_copy(value[:, :, 0], index[:, 0:2]))
            own(dve.scalar_tensor_tensor(key[:, :], value[:, :, 0], float(SLOTS), pair_no[:, :], ALU.mult, ALU.add))
            for k in range(2):
                last = dve.tensor_scalar(spread[:, :, k], ident[:, :], key[:, k:k + 1], None, ALU.mult)
            last.then_inc(s["spread_ready"], 1)
            dve.wait_ge(s["second_ready"], 1)
            own(dve.tensor_scalar(total[:, :], second[:, :], 1.0, None, ALU.add))
            own(dve.reciprocal(value[:, 0, 2:3], total[:, :]))
            dve.tensor_tensor(value[:, 1, 2:3], second[:, :], value[:, 0, 2:3], ALU.mult)
            dve.wait_ge(s["keys_ready"], 1)
            for k in range(2):
                last = dve.tensor_scalar(less[:, k, :], pk[0:B, 0:SLOTS], key[:, k:k + 1], None, ALU.is_lt)
            own(last)
            own(dve.tensor_reduce(rank[:, :], less[:, :, :], AX.X, ALU.add))
            for k in range(2):
                dve.tensor_scalar(chosen[:, k, :], slot_no[:, :], rank[:, k:k + 1], None, ALU.is_equal)
            dve.tensor_copy(wide[:, :, :, :].rearrange("b k c p -> b (k c) p"), value[:, :, :].rearrange("b k c -> b (k c)")
                            .unsqueeze(2).to_broadcast([B, 6, P])).then_inc(s["wide_ready"], 1)
            dve.wait_ge(s["table_ready"], 1)
            dve.tensor_copy(table[:, :, :], pt[:, 0:3 * SLOTS].rearrange("p (c s) -> p c s", c=3))
            dve.tensor_copy(etab[:, :], pt[0:1, 0:SLOTS])
            dve.tensor_copy(btab[:, :], pt[0:1, SLOTS:2 * SLOTS])


def experts(nc, x2, x2T, pooled_in, wr, w1, b1, w2, b2, out):
    with ExitStack() as ctx:
        def sb(name, shape, dt=F32):
            return ctx.enter_context(nc.sbuf_tensor("e_" + name, shape, dt))

        def sem(name):
            return ctx.enter_context(nc.semaphore("e_" + name))

        def banks(name, n):
            return [ctx.enter_context(nc.psum_tensor(f"e_{name}{i}", [P, 512], F32)) for i in range(n)]

        table = sb("table", [P, 3, SLOTS])
        etab, btab = sb("etab", [1, SLOTS], I32), sb("btab", [1, SLOTS], I32)
        b1T = sb("b1T", [P, E, FF // P])
        half = sb("half", [P, T])
        b1rows = sb("b1rows", [P, P])
        ident = sb("ident", [P, P])
        H_ps, Y_ps = banks("H", 4), banks("Y", 2)
        assert E * FF // P == P
        route(nc, pooled_in, wr, H_ps, table, etab, btab)

        with ExitStack() as sctx:
            b1_in, made, turned = [sctx.enter_context(nc.semaphore("e_" + n)) for n in ("b1_in", "made", "turned")]
            block = sctx.enter_context(nc.Block())

            @block.sync
            def _(sp):
                sp.dma_start(b1rows[:, :], b1.rearrange("e (t p) -> (e t) p", p=P)).then_inc(b1_in, 16)

            @block.gpsimd
            def _(pool):
                pool.memset(half[:, :], -0.5)
                pool.memset(ident[:, :], 0.0).then_inc(made, 1)
                pool.wait_ge(made, 1)
                pool.affine_select(ident[:, :], ident[:, :], [[-1, P]], ALU.not_equal, 1.0, base=0, channel_multiplier=1).then_inc(made, 1)

            @block.tensor
            def _(pe):
                pe.wait_ge(b1_in, 16)
                pe.wait_ge(made, 2)
                pe.transpose(H_ps[0][:, 0:P], b1rows[:, :], ident[:, :]).then_inc(turned, 1)

            @block.vector
            def _(dve):
                dve.wait_ge(turned, 1)
                dve.tensor_copy(b1T[:, :, :], H_ps[0][:, 0:P].rearrange("p (e t) -> p e t", e=E))

        raw = [sb(f"raw{i}", [P, 4, 512]) for i in range(RING)]
        wh = {"w1": [sb(f"w1h{c}", [P, KT, 512], F32R) for c in range(FC)], "w2": [sb(f"w2h{c}", [P, FT, D], F32R) for c in range(FC)]}
        wl = {"w1": [sb(f"w1l{c}", [P, KT, 512], F32R) for c in range(FC)], "w2": [sb(f"w2l{c}", [P, FT, D], F32R) for c in range(FC)]}
        xraw = sb("xraw", [P, KT, L])
        xh, xl = sb("xh", [P, KT, L], F32R), sb("xl", [P, KT, L], F32R)
        hf = [sb(f"hf{j}", [P, 2, L]) for j in range(2)]
        hh = [sb(f"hh{i}", [P, FT, L], F32R) for i in range(2)]
        hl = [sb(f"hl{i}", [P, FT, L], F32R) for i in range(2)]
        b1cur = sb("b1cur", [P, FF // P])
        b2cur = sb("b2cur", [P, D])
        wcur = sb("wcur", [P, 1])
        acc = sb("acc", [P, T, D])
        res = sb("res", [P, T, D])
        bn, mv, ve, rstd = sb("bn", [P, T, 6]), sb("mv", [P, T, 2]), sb("ve", [P, T]), sb("rstd", [P, T])

        names = ["x_in", "x_hi", "x_lo", "b2_in", "w_hi", "w_lo", "h_ready", "gelu_done", "h_hi", "h_lo", "y_done",
                 "b1_ready", "weight_ready", "acc_in", "acc_done", "res_done", "base_ready", "y_read", "stat", "res_ready",
                 "own_dve", "own_pool", "stood"]
        s = {n: sem(n) for n in names}
        w_in = [sem(f"w_in{i}") for i in range(RING)]
        block = ctx.enter_context(nc.Block())

        def used(n, chunk):
            kind, c = chunk
            return 8 * (n - 1) + 2 * c + 2 if kind == "w1" else FC * (n - 1) + c + 1

        def chunk_no(n, chunk):
            return 8 * n + CHUNKS.index(chunk)

        @block.sync
        def _(sp):
            def load_chunk(n, e, chunk):
                kind, c = chunk
                k = CHUNKS.index(chunk) % RING
                sp.wait_ge(s["w_lo"], chunk_no(n, chunk) + 1)
                if kind == "w1":
                    src = w1[e].rearrange("(k p) f -> p k f", p=P)[:, :, c * 512:(c + 1) * 512]
                else:
                    src = w2[e].rearrange("(c a p) d -> c p a d", a=FT, p=P)[c]
                sp.dma_start(raw[k][:, :, :], src).then_inc(w_in[k], 16)

            def slot(n):
                e = sp.value_load(etab[0:1, bass.ds(n, 1)], min_val=0, max_val=E - 1)
                b = sp.value_load(btab[0:1, bass.ds(n, 1)], min_val=0, max_val=B - 1)
                sp.wait_ge(s["x_lo"], n + 1)
                sp.dma_start(xraw[:, :, :], x2T[b + 1]).then_inc(s["x_in"], 16)
                for chunk in CHUNKS:
                    load_chunk(n, e, chunk)
                sp.wait_ge(s["base_ready"], n + 1)
                sp.dma_start(b2cur[:, :], b2[e].partition_broadcast(P)).then_inc(s["b2_in"], 16)

            with sp.Fori(0, SLOTS) as n:
                slot(n)

        @block.gpsimd
        def _(pool):
            def fetch_b1(n):
                e = pool.value_load(etab[0:1, bass.ds(n, 1)], min_val=0, max_val=E - 1)
                pool.wait_ge(s["gelu_done"], 8 * n + 4)
                pool.sem_inc(s["stood"], 1)
                pool.tensor_copy(b1cur[:, :], b1T[:, bass.ds(e, 1), :].rearrange("p o t -> p (o t)")).then_inc(s["b1_ready"], 1)

            def slot(n, more):
                b = pool.value_load(btab[0:1, bass.ds(n, 1)], min_val=0, max_val=B - 1)
                if not (isinstance(n, int) and n == 0):
                    stand(pool, s["acc_done"], 16 * n, s["stood"])
                pool.dma_start(acc[:, :, :], x2[b + 1].rearrange("(t p) d -> p t d", p=P)).then_inc(s["acc_in"], 16)
                pool.tensor_copy(wcur[:, :], table[:, 2, bass.ds(n, 1)]).then_inc(s["weight_ready"], 1)
                if more:
                    fetch_b1(n + 1)
                stand(pool, s["stat"], n + 1, s["stood"])
                pool.dma_start(x2[b + 1].rearrange("(t p) d -> p t d", p=P), acc[:, :, :]).then_inc(s["acc_done"], 16)
                pool.tensor_scalar(ve[:, :], mv[:, :, 1], EPS, None, ALU.add).then_inc(s["own_pool"], 1)
                pool.wait_ge(s["own_pool"], 2 * n + 1)
                pool.tensor_tensor(rstd[:, :], ve[:, :], half[:, :], ALU.pow).then_inc(s["own_pool"], 1)
                stand(pool, s["own_pool"], 2 * n + 2, s["stood"])
                if not (isinstance(n, int) and n == 0):
                    stand(pool, s["res_done"], 16 * n, s["stood"])
                for t in range(T):
                    last = pool.tensor_scalar(res[:, t, :], acc[:, t, :], mv[:, t, 0:1], rstd[:, t:t + 1], ALU.subtract, ALU.mult)
                last.then_inc(s["res_ready"], 1)
                stand(pool, s["res_ready"], n + 1, s["stood"])
                pool.dma_start(out[b].rearrange("(t p) d -> p t d", p=P), res[:, :, :]).then_inc(s["res_done"], 16)

            fetch_b1(0)
            slot(0, True)
            with pool.Fori(1, SLOTS - 1) as n:
                slot(n, True)
            slot(SLOTS - 1, False)
            pool.wait_ge(s["acc_done"], 16 * SLOTS)
            pool.wait_ge(s["res_done"], 16 * SLOTS)

        @block.scalar
        def _(act):
            act.sem_inc(s["gelu_done"], 4)

            def split(n, chunk):
                kind, c = chunk
                k = CHUNKS.index(chunk)
                act.wait_ge(w_in[k % RING], 16 * (8 // RING * n + k // RING + 1))
                act.activation(wh[kind][c][:, :, :], raw[k % RING][:, :, :], ACT.Copy).then_inc(s["w_hi"], 1)

            def hidden(n, c):
                if c == 0:
                    act.wait_ge(s["b1_ready"], n + 1)
                for j in range(2):
                    g = 2 * (FC * n + c) + j
                    act.wait_ge(s["h_ready"], g + 1)
                    act.wait_ge(s["h_lo"], g + 1)
                    for a in range(2):
                        last = act.activation(hf[j][:, a, :], H_ps[2 * (c % 2) + j][:, a * L:(a + 1) * L], ACT.Gelu,
                                              bias=b1cur[:, FT * c + 2 * j + a:FT * c + 2 * j + a + 1])
                    last.then_inc(s["gelu_done"], 1)
                for j in range(2):
                    g = 2 * (FC * n + c) + j
                    act.wait_ge(s["gelu_done"], g + 5)
                    act.activation(hh[c % 2][:, 2 * j:2 * j + 2, :], hf[j][:, :, :], ACT.Copy).then_inc(s["h_hi"], 1)

            def body(n, order):
                for kind, i in order:
                    if kind == "h":
                        hidden(n, i)
                    elif kind == "nh":
                        hidden(n + 1, 0)
                    elif kind == "split":
                        if not (isinstance(n, int) and n == 0):
                            act.wait_ge(s["y_done"], used(n, i))
                        split(n, i)
                    elif kind == "nsplit":
                        if not (isinstance(n, int) and n == -1):
                            used_by = s["y_done"] if i[0] == "w2" else s["h_ready"]
                            act.wait_ge(used_by, used(n + 1, i))
                        split(n + 1, i)
                    elif kind == "nx":
                        if not (isinstance(n, int) and n == -1):
                            act.wait_ge(s["h_ready"], 8 * n + 8)
                        act.wait_ge(s["x_in"], 16 * (n + 2))
                        act.activation(xh[:, :, :], xraw[:, :, :], ACT.Copy).then_inc(s["x_hi"], 1)

            body(-1, FIRST3)
            body(0, ORDER3)
            with act.Fori(1, SLOTS - 1) as n:
                body(n, ORDER3)
            body(SLOTS - 1, LAST3)

        @block.vector
        def _(dve):
            dve.sem_inc(s["w_lo"], RING)
            dve.sem_inc(s["x_lo"], 1)
            dve.sem_inc(s["h_lo"], 2)
            dve.sem_inc(s["base_ready"], 1)
            dve.sem_inc(s["y_read"], 1)

            def split(n, chunk):
                kind, c = chunk
                k = CHUNKS.index(chunk)
                dve.wait_ge(s["w_hi"], chunk_no(n, chunk) + 1)
                dve.tensor_tensor(wl[kind][c][:, :, :], raw[k % RING][:, :, :], fp(wh[kind][c][:, :, :]), ALU.subtract).then_inc(s["w_lo"], 1)

            def hidden(n, c):
                for j in range(2):
                    g = 2 * (FC * n + c) + j
                    dve.wait_ge(s["h_hi"], g + 1)
                    dve.tensor_tensor(hl[c % 2][:, 2 * j:2 * j + 2, :], hf[j][:, :, :], fp(hh[c % 2][:, 2 * j:2 * j + 2, :]),
                                      ALU.subtract).then_inc(s["h_lo"], 1)

            def body(n, order):
                for kind, i in order:
                    if kind == "h":
                        hidden(n, i)
                    elif kind == "nh":
                        hidden(n + 1, 0)
                    elif kind == "split":
                        split(n, i)
                    elif kind == "nsplit":
                        split(n + 1, i)
                    elif kind == "nx":
                        dve.wait_ge(s["x_hi"], n + 2)
                        dve.tensor_tensor(xl[:, :, :], xraw[:, :, :], fp(xh[:, :, :]), ALU.subtract).then_inc(s["x_lo"], 1)
                    elif kind == "base":
                        dve.wait_ge(s["acc_in"], 16 * (n + 1))
                        dve.wait_ge(s["b2_in"], 16 * (n + 1))
                        dve.wait_ge(s["weight_ready"], n + 1)
                        for t in range(T):
                            last = dve.scalar_tensor_tensor(acc[:, t, :], b2cur[:, :], wcur[:, 0:1], acc[:, t, :], ALU.mult, ALU.add)
                        last.then_inc(s["base_ready"], 1)
                    elif kind == "end":
                        dve.wait_ge(s["base_ready"], n + 2)
                        dve.wait_ge(s["y_done"], FC * (n + 1))
                        for t in range(T):
                            last = dve.scalar_tensor_tensor(acc[:, t, :], Y_ps[t][:, :], wcur[:, 0:1], acc[:, t, :], ALU.mult, ALU.add)
                        last.then_inc(s["y_read"], 1)
                        dve.wait_ge(s["y_read"], n + 2)
                        for t in range(T):
                            last = dve.bn_stats(bn[:, t, :], acc[:, t, :])
                        last.then_inc(s["own_dve"], 1)
                        stand(dve, s["own_dve"], n + 1, s["stood"])
                        for t in range(T):
                            last = dve.bn_aggr(mv[:, t, :], bn[:, t, :])
                        last.then_inc(s["stat"], 1)

            body(-1, FIRST3)
            with dve.Fori(0, SLOTS - 1) as n:
                body(n, ORDER3)
            body(SLOTS - 1, LAST3)

        @block.tensor
        def _(pe):
            def hidden(n, c):
                pe.wait_ge(s["w_lo"], chunk_no(n, ("w1", c)) + RING + 1)
                if c == 0:
                    pe.wait_ge(s["x_lo"], n + 2)
                for j in range(2):
                    g = 2 * (FC * n + c) + j
                    pe.wait_ge(s["gelu_done"], g + 1)
                    for a in range(2):
                        f = slice((2 * j + a) * P, (2 * j + a + 1) * P)
                        for k in range(KT):
                            last = product3(pe, H_ps[2 * (c % 2) + j][:, a * L:(a + 1) * L], (wh["w1"][c][:, k, f], wl["w1"][c][:, k, f]),
                                            (xh[:, k, :], xl[:, k, :]), k == 0, k == KT - 1)
                    last.then_inc(s["h_ready"], 1)

            def result(n, c):
                pe.wait_ge(s["w_lo"], chunk_no(n, ("w2", c)) + RING + 1)
                pe.wait_ge(s["h_lo"], 2 * (FC * n + c) + 4)
                if c == 0:
                    pe.wait_ge(s["y_read"], n + 1)
                for a in range(FT):
                    for t in range(T):
                        q = slice(t * P, (t + 1) * P)
                        last = product3(pe, Y_ps[t][:, :], (hh[c % 2][:, a, q], hl[c % 2][:, a, q]), (wh["w2"][c][:, a, :], wl["w2"][c][:, a, :]),
                                        c == 0 and a == 0, c == FC - 1 and a == FT - 1)
                last.then_inc(s["y_done"], 1)

            def body(n, order):
                for kind, i in order:
                    if kind == "h":
                        hidden(n, i)
                    elif kind == "nh":
                        hidden(n + 1, 0)
                    elif kind == "y":
                        result(n, i)

            body(-1, FIRST3)
            with pe.Fori(0, SLOTS - 1) as n:
                body(n, ORDER3)
            body(SLOTS - 1, LAST3)


def rope_tables():
    import numpy as np
    inv = (1.0 / np.float32(10000.0) ** (np.arange(0, D1, 2, dtype=np.float32) / np.float32(D1))).astype(np.float32)
    ang = (np.arange(L, dtype=np.float32)[:, None] * inv[None, :]).astype(np.float32).astype(np.float64)
    cos, sin = np.repeat(np.cos(ang), 2, axis=1), np.repeat(np.sin(ang), 2, axis=1)
    sin[:, 0::2] *= -1
    tab = np.stack([cos, sin]).reshape(2, T, P, D1)
    tab = np.stack([tab / np.sqrt(D1), tab])
    return np.ascontiguousarray(tab.transpose(3, 0, 1, 2, 4)).astype(np.float32)



ATTN = ["ln_gamma", "ln_beta", "Wq", "bq", "Wk", "bk", "Wv", "bv", "Wo", "bo"]
NAMES = (["x", "ctx_1024"] + ["L0_attn_" + n for n in ATTN] + ["L0_xattn_W" + c for c in "qkvo"]
         + ["L0_ffn_" + n for n in ("Wr", "W1", "b1", "W2", "b2")])


def decoder_layer(nc, a, out):
    x1 = nc.dram_tensor("x1", (B + 1, L, D), F32).ap()
    x2 = nc.dram_tensor("x2", (B + 1, L, D), F32).ap()
    x2T = nc.dram_tensor("x2T", (B + 1, P, KT, L), F32).ap()
    pooled = nc.dram_tensor("pooled", (P, KT, B + 1), F32).ap()
    self_attention(nc, a["x"], a["L0_attn_ln_gamma"], a["L0_attn_ln_beta"], [a["L0_attn_W" + c] for c in "qkvo"],
                   [a["L0_attn_b" + c] for c in "qkvo"], a["rope"], x1)
    cross_attention(nc, x1, a["ctx_1024"], [a["L0_xattn_W" + c] for c in "qkvo"], x2, x2T, pooled)
    experts(nc, x2, x2T, pooled, a["L0_ffn_Wr"], a["L0_ffn_W1"], a["L0_ffn_b1"], a["L0_ffn_W2"], a["L0_ffn_b2"], out)


def kernel(**inputs):
    import numpy as _np
    import concourse.bacc as _bacc
    from concourse import mybir as _mybir
    from concourse.bass_utils import run_bass_kernel_spmd as _run

    nc = _bacc.Bacc("TRN2", target_bir_lowering=False, num_devices=1)
    given = {name: inputs[name] for name in NAMES}
    given["rope"] = rope_tables()
    arrays, a = {}, {}
    for name, value in given.items():
        value = _np.ascontiguousarray(value)
        arrays[f"in_{name}_dram"] = value
        a[name] = nc.dram_tensor(f"in_{name}_dram", value.shape, _mybir.dt.from_np(value.dtype), kind="ExternalInput").ap()
    out = nc.dram_tensor("out_0_dram", (B, L, D), F32, kind="ExternalOutput").ap()
    decoder_layer(nc, a, out)
    r = _run(nc, [arrays], core_ids=[0])
    return r.results[0]["out_0_dram"]
```

```python
from contextlib import ExitStack

import concourse.bass as bass
from concourse import mybir

P = 128
F32 = mybir.dt.float32
F32R = mybir.dt.float32r
BF16 = mybir.dt.bfloat16
I32 = mybir.dt.int32
ALU = mybir.AluOpType
ACT = mybir.ActivationFunctionType
AX = mybir.AxisListType
EPS = 1e-5
MASKED = -1e30

B, L, D = 16, 256, 512
T = L // P
KT = D // P
HEADS = 16
E = 8
FF = 2048
SLOTS = 2 * B


def fp(ap):
    return ap.bitcast(F32)


def product3(pe, out, stationary, moving, first, last):
    (sh, sl), (mh, ml) = stationary, moving
    pe.matmul(out, sh, mh, start=first, stop=False)
    pe.matmul(out, sh, ml, start=False, stop=False)
    return pe.matmul(out, sl, mh, start=False, stop=last)


class OwnSteps:

    def __init__(self, base=0):
        self.base, self.n = base, 0

    def next(self):
        self.n += 1
        return self.base + self.n


def stand(eng, sem, value, stood):
    eng.wait_ge(sem, value)
    eng.sem_inc(stood, 1)



D1 = D // HEADS

UNITS1 = []
for _g in range(4):
    UNITS1 += [(0, list(range(4 * _g, 4 * _g + 4)), _g), (1, [4 * _g, 4 * _g + 1], _g), (1, [4 * _g + 2, 4 * _g + 3], _g)]
NU1 = len(UNITS1)

ORDER1 = [("S", 0), ("pot", 0), ("pot", 1), ("split", 1), ("S", 1), ("S", 2), ("py", 0), ("T", 0), ("nz",), ("T", 1), ("S", 3),
          ("V", 0), ("nproj", 0), ("nstat", 2), ("T", 2), ("V", 1), ("T", 3), ("S", 4), ("S", 5), ("nproj", 1), ("nnorm", 2),
          ("V", 2), ("T", 4), ("V", 3), ("nstack", 0), ("nproj", 2), ("S", 6), ("T", 5), ("V", 4), ("nproj", 3), ("nstack", 1),
          ("S", 7), ("V", 5), ("T", 6), ("nstack", 2), ("nval", 0), ("T", 7), ("py", 1), ("V", 6), ("nstack", 3), ("S", 8),
          ("V", 7), ("S", 9), ("pstat",), ("T", 8), ("nturn", 0, 0), ("S", 10), ("nturn", 0, 1), ("T", 9), ("nturn", 1, 0),
          ("nturn", 1, 1), ("S", 11), ("V", 8), ("nturn", 2, 0), ("pnorm",), ("T", 10), ("V", 9), ("nturn", 2, 1), ("T", 11),
          ("nturn", 3, 0), ("V", 10), ("nturn", 3, 1), ("V", 11), ("nsplit", 0), ("nval", 1), ("base",)]
FIRST1 = ([("nstat", 1), ("nnorm", 1), ("nz",), ("nproj", 0), ("nproj", 1), ("nstack", 0), ("nproj", 2), ("nstack", 1), ("nproj", 3),
           ("nval", 0), ("nstat", 2), ("nstack", 2), ("nnorm", 2), ("nstack", 3)]
          + [("nturn", _g, _w) for _g in range(4) for _w in range(2)] + [("nsplit", 0), ("nval", 1)])
LAST1 = [st for st in ORDER1 if not st[0].startswith("n")]
FINISH1 = [("pot", 0), ("pot", 1), ("py", 0), ("py", 1), ("pstat",), ("pnorm",)]


def spare_uses(step):
    return {"nz": (T, "dve"), "nproj": (1, "dve"), "nturn": (2, "dve" if step[-1] else "act"), "nval": (1, "dve"),
            "pot": (1, "dve"), "py": (1, "dve")}.get(step[0], (0, "dve"))


def uses_in(steps, *released_by):
    return sum(n for n, by in map(spare_uses, steps) if by in released_by)


def after(order, step):
    return uses_in(order[order.index(step) + 1:], "dve")


class SpareBanks:

    def __init__(self, ready, by_dve, by_act):
        self.ready, self.n = ready, 0
        self.made = {"dve": by_dve, "act": by_act}
        self.past = [("dve", by_dve - 1), ("dve", by_dve)]

    def next(self, by):
        bank, before = self.n % 2, self.past[self.n]
        self.n += 1
        self.made[by] = self.made[by] + 1
        self.past.append((by, self.made[by]))
        return bank, self.ready + self.n, before


def self_attention(nc, x, gamma, beta, weights, biases, rope, x1, ahead):
    with ExitStack() as ctx:
        def sb(name, shape, dt=F32):
            return ctx.enter_context(nc.sbuf_tensor(name, shape, dt))

        def sem(name):
            return ctx.enter_context(nc.semaphore(name))

        def banks(name, n):
            return [ctx.enter_context(nc.psum_tensor(f"{name}{i}", [P, 512], F32)) for i in range(n)]

        halves = [[sb(f"a_w{e}{i}", [P, KT, D], F32R) for e in "hl"] for i in range(4)]
        wh, wl = [w[0] for w in halves], [w[1] for w in halves]
        bias = [sb(f"a_bias{i}", [P, D]) for i in range(4)]
        ident = sb("a_ident", [P, P])
        identb = sb("a_identb", [P, P], BF16)
        causal = sb("a_causal", [P, P], BF16)
        tables = sb("a_rope", [P, 2, 2, T, D1])
        half = sb("a_half", [P, T])
        acc = sb("a_acc", [P, T, D])
        o = sb("a_o", [P, T, D])
        xs = sb("a_xs", [P, T, D])

        names = ["xs_in", "acc_in", "out_done", "stat", "rstd_ready", "z_ready", "f_ready", "f_dve", "f_act", "z_hi",
                 "turned_ready", "turned_hi", "turned_lo", "v_hi", "v_lo",
                 "s_ready", "max_ready", "exp_done", "t_ready", "p_hi", "p_lo", "pv_done", "o_ready",
                 "ot_hi", "base_ready", "stat2", "rstd2_ready", "out_ready", "own_dve", "own_pool", "stood"]
        s = {n: sem("a_" + n) for n in names}

        S_ps, T_ps, O_ps, F_ps = banks("a_S", 2), banks("a_T", 2), banks("a_O", 2), banks("a_F", 2)

        with ExitStack() as sctx:
            raw = [sctx.enter_context(nc.sbuf_tensor(f"a_raw{i}", [P, KT, D], F32)) for i in range(4)]
            scaled = [sctx.enter_context(nc.sbuf_tensor(f"a_scaled{i}", [P, KT, D], F32)) for i in range(3)]
            gcol = sctx.enter_context(nc.sbuf_tensor("a_gcol", [P, KT], F32))
            bcol = sctx.enter_context(nc.sbuf_tensor("a_bcol", [P, KT], F32))
            brep = sctx.enter_context(nc.sbuf_tensor("a_brep", [P, KT, P], F32))
            w_in = [sctx.enter_context(nc.semaphore(f"a_w_in{i}")) for i in range(4)]
            cols_in = sctx.enter_context(nc.semaphore("a_cols_in"))
            small_in = sctx.enter_context(nc.semaphore("a_small_in"))
            made = sctx.enter_context(nc.semaphore("a_made"))
            w_scaled = sctx.enter_context(nc.semaphore("a_w_scaled"))
            w_hi = sctx.enter_context(nc.semaphore("a_w_hi"))
            rep_ready = sctx.enter_context(nc.semaphore("a_rep_ready"))
            bw_ready = sctx.enter_context(nc.semaphore("a_bw_ready"))
            block = sctx.enter_context(nc.Block())

            @block.sync
            def _(sp):
                with nc.allow_non_contiguous_dma("gamma and beta as columns, once"):
                    sp.dma_start(gcol[:, :], gamma.rearrange("(t p) -> p t", p=P)).then_inc(cols_in, 16)
                    sp.dma_start(bcol[:, :], beta.rearrange("(t p) -> p t", p=P)).then_inc(cols_in, 16)
                for i in range(4):
                    sp.dma_start(raw[i][:, :, :], weights[i].rearrange("(t p) n -> p t n", p=P)).then_inc(w_in[i], 16)
                for i in range(4):
                    sp.dma_start(bias[i][:, :], biases[i].partition_broadcast(P)).then_inc(small_in, 16)
                sp.dma_start(tables[:, :, :, :, :], rope).then_inc(small_in, 16)
                sp.dma_start(xs[:, :, :], x[0].rearrange("(t p) d -> p t d", p=P)).then_inc(s["xs_in"], 16)
                sp.wait_ge(small_in, 16 * 5)

            @block.gpsimd
            def _(pool):
                pool.memset(ident[:, :], 0.0).then_inc(made, 1)
                pool.memset(identb[:, :], 0.0).then_inc(made, 1)
                pool.memset(causal[:, :], 0.0).then_inc(made, 1)
                pool.memset(half[:, :], -0.5)
                pool.memset(acc[:, :, :], 0.0)
                pool.memset(o[:, :, :], 0.0)
                pool.wait_ge(made, 3)
                pool.affine_select(ident[:, :], ident[:, :], [[-1, P]], ALU.not_equal, 1.0, base=0, channel_multiplier=1)
                pool.affine_select(identb[:, :], identb[:, :], [[-1, P]], ALU.not_equal, 1.0, base=0, channel_multiplier=1)
                pool.affine_select(causal[:, :], causal[:, :], [[-1, P]], ALU.is_ge, MASKED, base=0, channel_multiplier=1)

            @block.vector
            def _(dve):
                dve.wait_ge(cols_in, 32)
                dve.tensor_copy(brep[:, :, :], bcol[:, :].unsqueeze(2).to_broadcast([P, KT, P])).then_inc(rep_ready, 1)

                def scale(i):
                    dve.wait_ge(w_in[i], 16)
                    for t in range(KT):
                        last = dve.tensor_scalar(scaled[i][:, t, :], raw[i][:, t, :], gcol[:, t:t + 1], None, ALU.mult)
                    last.then_inc(w_scaled, 1)

                scale(0)
                for i in range(4):
                    if i < 2:
                        scale(i + 1)
                    if i == 3:
                        dve.wait_ge(w_in[3], 16)
                    dve.wait_ge(w_hi, i + 1)
                    dve.tensor_tensor(wl[i][:, :, :], (raw[3] if i == 3 else scaled[i])[:, :, :], fp(wh[i][:, :, :]), ALU.subtract)
                dve.wait_ge(small_in, 16 * 5)
                for i in range(3):
                    dve.wait_ge(bw_ready, i + 1)
                    dve.tensor_tensor(bias[i][:, :], (F_ps[0], F_ps[1], S_ps[0])[i][:, :], bias[i][:, :], ALU.add)
                dve.tensor_scalar(bias[3][:, :], bias[3][:, :], 0.5, None, ALU.mult)

            @block.scalar
            def _(act):
                for i in range(4):
                    act.wait_ge(w_in[i], 16)
                    if i < 3:
                        act.wait_ge(w_scaled, i + 1)
                    act.activation(wh[i][:, :, :], (raw[i] if i == 3 else scaled[i])[:, :, :], ACT.Copy).then_inc(w_hi, 1)

            @block.tensor
            def _(pe):
                pe.wait_ge(rep_ready, 1)
                for i in range(3):
                    pe.wait_ge(w_in[i], 16)
                    bank = (F_ps[0], F_ps[1], S_ps[0])[i]
                    for t in range(KT):
                        last = pe.matmul(bank[:, :], brep[:, t, :], raw[i][:, t, :], start=t == 0, stop=t == KT - 1)
                    last.then_inc(bw_ready, 1)

        zh, zl = sb("a_zh", [P, KT, L], F32R), sb("a_zl", [P, KT, L], F32R)
        biased = [sb(f"a_biased{i}", [P, D]) for i in range(2)]
        turn_cos, turn_sin = sb("a_turn_cos", [P, D]), sb("a_turn_sin", [P, D])
        turned = [sb(f"a_turned{i}", [P, D]) for i in range(2)]
        stack = [[sb(f"a_stack{i}{t}", [P, HEADS, 4, D1], F32R) for t in range(T)] for i in range(2)]
        stackT = [sb(f"a_stackT{i}", [P, HEADS, L], F32R) for i in range(2)]
        v = [sb(f"a_v{t}", [P, HEADS, 2, D1], F32R) for t in range(T)]
        vfull = [sb(f"a_vfull{t}", [P, D]) for t in range(T)]
        negmax = sb("a_negmax", [P, 2, 4])
        probs = [sb(f"a_probs{i}", [P, 512]) for i in range(2)]
        sums = sb("a_sums", [P, T, HEADS])
        pTh = [sb(f"a_pTh{i}", [P, 4, P], F32R) for i in range(2)]
        pTl = [sb(f"a_pTl{i}", [P, 4, P], F32R) for i in range(2)]
        rsum = sb("a_rsum", [P, T, 4])
        osum = sb("a_osum", [P, T, 4, D1])
        oTh = [sb(f"a_oTh{t}", [P, KT, P], F32R) for t in range(T)]
        oTl = [sb(f"a_oTl{t}", [P, KT, P], F32R) for t in range(T)]
        bn = sb("a_bn", [P, 2, T, 6])
        mv = sb("a_mv", [P, 2, T, 2])
        ve = sb("a_ve", [P, 2, T])
        rstd = sb("a_rstd", [P, 2, T])

        block = ctx.enter_context(nc.Block())

        def spare(b, order=()):
            return SpareBanks(*(uses_in(FIRST1, *by) + uses_in(ORDER1, *by) * b + uses_in(order, *by)
                                for by in (("dve", "act"), ("dve",), ("act",))))

        def spare_first():
            return SpareBanks(0, 0, 0)

        def spare_last():
            return spare(B - 1, LAST1)

        def wait_spare(eng, before, first):
            by, count = before
            if not (first and isinstance(count, int) and count <= 0):
                eng.wait_ge(s["f_" + by], count)

        @block.sync
        def _(sp):
            def load_xs(b, transposed):
                sp.wait_ge(s["f_ready"], transposed)
                sp.dma_start(xs[:, :, :], x[b].rearrange("(t p) d -> p t d", p=P)).then_inc(s["xs_in"], 16)

            def store(b):
                sp.wait_ge(s["out_ready"], b + 2)
                sp.dma_start(x1[b + 1].rearrange("(t p) d -> p t d", p=P), acc[:, :, :]).then_inc(s["out_done"], 16)

            def load_acc(b):
                sp.wait_ge(s["out_done"], 16 * (b + 1))
                sp.dma_start(acc[:, :, :], x[b].rearrange("(t p) d -> p t d", p=P)).then_inc(s["acc_in"], 16)

            to_nz = ORDER1[:ORDER1.index(("nz",)) + 1]
            load_xs(1, T)
            with sp.Fori(0, B - 2) as b:
                load_xs(b + 2, spare(b, to_nz).ready)
                store(b - 1)
                load_acc(b)
            load_xs(B - 1, spare(B - 2, to_nz).ready)
            for b in (B - 2, B - 1):
                store(b - 1)
                load_acc(b)
            sp.wait_ge(s["f_ready"], spare(B - 1).ready)
            for destination, source, arrived in ahead:
                sp.dma_start(destination, source).then_inc(arrived, 16)
            store(B - 1)
            sp.wait_ge(s["out_done"], 16 * (B + 1))

        @block.gpsimd
        def _(pool):
            pool.sem_inc(s["turned_ready"], 2)
            pool.sem_inc(s["base_ready"], 1)

            def rsqrt(own, which, ready):
                pool.tensor_scalar(ve[:, which, :], mv[:, which, :, 1], EPS, None, ALU.add).then_inc(s["own_pool"], 1)
                pool.wait_ge(s["own_pool"], own.next())
                pool.tensor_tensor(rstd[:, which, :], ve[:, which, :], half[:, :], ALU.pow).then_inc(ready, 1)

            def turn(own, by_dve, n, i):
                t, w = i // 2, i % 2
                b4 = biased[i % 2][:, :].rearrange("p (h m e) -> p h m e", h=HEADS, e=2)
                sn = turn_sin[:, :].rearrange("p (h m e) -> p h m e", h=HEADS, e=2)
                cos = tables[:, w, 0, t, :].unsqueeze(1).to_broadcast([P, HEADS, D1])
                sin = tables[:, w, 1, t, :].rearrange("p (m e) -> p m e", e=2)
                pool.wait_ge(s["f_dve"], by_dve)
                pool.wait_ge(s["turned_ready"], n + 1)
                pool.tensor_tensor(turn_cos[:, :].rearrange("p (h d) -> p h d", h=HEADS),
                                   biased[i % 2][:, :].rearrange("p (h d) -> p h d", h=HEADS), cos, ALU.mult)
                for e in range(2):
                    last = pool.tensor_tensor(sn[:, :, :, e], b4[:, :, :, 1 - e],
                                              sin[:, :, e].unsqueeze(1).to_broadcast([P, HEADS, D1 // 2]), ALU.mult)
                last.then_inc(s["own_pool"], 1)
                pool.wait_ge(s["turned_lo"], n)
                pool.wait_ge(s["own_pool"], own.next())
                pool.tensor_tensor(turned[i % 2][:, :], turn_cos[:, :], turn_sin[:, :], ALU.add).then_inc(s["turned_ready"], 1)

            def body(b, order, ring, own):
                for step in order:
                    n, by = spare_uses(step)
                    for _ in range(n):
                        ring.next(by)
                    if step[0] == "nstat":
                        stand(pool, s["stat"], b + step[1] + 1, s["stood"])
                        rsqrt(own, 0, s["rstd_ready"])
                    elif step[0] == "nproj":
                        i = step[1]
                        turn(own, ring.made["dve"], 4 * (b + 1) + i + 1, i)
                    elif step[0] == "pstat":
                        stand(pool, s["stat2"], b + 1, s["stood"])
                        rsqrt(own, 1, s["rstd2_ready"])
                    elif step[0] == "base":
                        pool.wait_ge(s["acc_in"], 16 * (b + 1))
                        pool.tensor_tensor(acc[:, :, :], acc[:, :, :], bias[3][:, :].unsqueeze(1).to_broadcast([P, T, D]),
                                           ALU.add).then_inc(s["base_ready"], 1)

            per_body = 1 + 4 + 1
            body(-1, FIRST1, spare_first(), OwnSteps())
            with pool.Fori(0, B - 1) as b:
                body(b, ORDER1, spare(b), OwnSteps(6 + per_body * b))
            body(B - 1, LAST1, spare(B - 1), OwnSteps(6 + per_body * (B - 1)))
            body(B, FINISH1, spare_last(), OwnSteps(6 + per_body * (B - 1) + 1))

        @block.scalar
        def _(act):
            act.sem_inc(s["exp_done"], 2)

            def body(b, order, ring):
                u0 = NU1 * b
                for step in order:
                    n, by = spare_uses(step)
                    uses = [ring.next(by) for _ in range(n)]
                    if step[0] == "S":
                        u = step[1]
                        t, heads, g = UNITS1[u]
                        act.wait_ge(s["max_ready"], u0 + u + 1)
                        act.wait_ge(s["t_ready"], u0 + u + 1)
                        nj = P * (t + 1)
                        for j, h in enumerate(heads):
                            last = act.activation(probs[u % 2][:, j * nj:(j + 1) * nj], S_ps[u % 2][:, j * nj:(j + 1) * nj],
                                                  ACT.Exp, bias=negmax[:, u % 2, j:j + 1], accum_out=sums[:, t, h:h + 1])
                        last.then_inc(s["exp_done"], 1)
                    elif step[0] == "T":
                        u = step[1]
                        act.wait_ge(s["t_ready"], u0 + u + 3)
                        act.wait_ge(s["pv_done"], u0 + u + 1)
                        act.activation(pTh[u % 2][:, :, :], T_ps[u % 2][:, :], ACT.Copy).then_inc(s["p_hi"], 1)
                    elif step[0] == "nz":
                        for j, (bank, ready, _) in enumerate(uses):
                            act.wait_ge(s["f_ready"], ready)
                            act.activation(zh[:, 2 * j:2 * j + 2, :], F_ps[bank][:, :], ACT.Copy).then_inc(s["z_hi"], 1)
                    elif step[0] == "nstack":
                        i = step[1]
                        w, t = i % 2, i // 2
                        act.wait_ge(s["turned_ready"], 4 * (b + 1) + i + 3)
                        places = stack[w][t][:, :, 0:2, :] if w == 0 else stack[w][t][:, :, 0:4:2, :]
                        act.activation(places, turned[i % 2][:, :].rearrange("p (h d) -> p h d", h=HEADS).unsqueeze(2)
                                       .to_broadcast([P, HEADS, 2, D1]), ACT.Copy).then_inc(s["turned_hi"], 1)
                    elif step[0] == "nturn":
                        g, w = step[1:]
                        for t, (bank, ready, _) in enumerate(uses if w == 0 else []):
                            act.wait_ge(s["f_ready"], ready)
                            act.activation(stackT[w][:, 4 * g:4 * g + 4, t * P:(t + 1) * P], F_ps[bank][:, :]
                                           .rearrange("p (h q) -> p h q", h=4), ACT.Copy).then_inc(s["f_act"], 1)
                    elif step == ("nval", 0):
                        filled = ring.made["dve"]
                    elif step[0] in ("split", "nsplit"):
                        t = step[1]
                        act.wait_ge(s["pv_done"], NU1 * (b + (step[0] == "nsplit")) + 2)
                        act.wait_ge(s["f_dve"], filled if t == 0 else spare(b).made["dve"] - after(ORDER1, ("nval", 1)))
                        act.activation(v[t][:, :, 0, :], vfull[t][:, :].rearrange("p (h d) -> p h d", h=HEADS), ACT.Copy).then_inc(s["v_hi"], 1)
                    elif step[0] == "pot":
                        t = step[1]
                        bank, ready, _ = uses[0]
                        act.wait_ge(s["f_ready"], ready)
                        act.activation(oTh[t][:, :, :], F_ps[bank][:, :], ACT.Copy).then_inc(s["ot_hi"], 1)

            body(-1, FIRST1, spare_first())
            with act.Fori(0, B - 1) as b:
                body(b, ORDER1, spare(b))
            body(B - 1, LAST1, spare(B - 1))
            body(B, FINISH1, spare_last())

        @block.vector
        def _(dve):
            dve.sem_inc(s["turned_lo"], 2)
            dve.sem_inc(s["v_lo"], 2)
            dve.sem_inc(s["p_lo"], 2)
            dve.sem_inc(s["o_ready"], 2)

            def own_step(own, last):
                last.then_inc(s["own_dve"], 1)
                stand(dve, s["own_dve"], own.next(), s["stood"])

            def outputs(b, g, own):
                dve.wait_ge(s["pv_done"], NU1 * b + 3 * g + 3 + 2)
                dve.wait_ge(s["o_ready"], 4 * b + g + 2)
                dve.reciprocal(rsum[:, :, :], sums[:, :, 4 * g:4 * g + 4])
                own_step(own, dve.tensor_reduce(osum[:, :, :, :].rearrange("p t h d -> p (t h) d"), O_ps[g % 2][:, :]
                                                .rearrange("p (g e d) -> p g d e", e=2, d=D1), AX.X, ALU.add))
                dve.tensor_tensor(o[:, :, 4 * D1 * g:4 * D1 * (g + 1)].rearrange("p t (h d) -> p t h d", h=4), osum[:, :, :, :],
                                  rsum[:, :, :].unsqueeze(3).to_broadcast([P, T, 4, D1]), ALU.mult).then_inc(s["o_ready"], 1)

            def body(b, order, ring, own):
                u0 = NU1 * b
                for step in order:
                    n, by = spare_uses(step)
                    uses = [ring.next(by) for _ in range(n)]
                    if step[0] == "S":
                        u = step[1]
                        t, heads, g = UNITS1[u]
                        dve.wait_ge(s["s_ready"], u0 + u + 1)
                        dve.wait_ge(s["exp_done"], u0 + u + 1)
                        dve.tensor_reduce(negmax[:, u % 2, 0:len(heads)], S_ps[u % 2][:, :]
                                          .rearrange("p (h j) -> p h j", h=len(heads)), AX.X, ALU.max, negate=True).then_inc(s["max_ready"], 1)
                    elif step[0] == "T":
                        u = step[1]
                        dve.wait_ge(s["p_hi"], u0 + u + 1)
                        dve.tensor_tensor(pTl[u % 2][:, :, :], T_ps[u % 2][:, :].rearrange("p (a q) -> p a q", a=4), fp(pTh[u % 2][:, :, :]), ALU.subtract).then_inc(s["p_lo"], 1)
                    elif step[0] == "V":
                        if step[1] % 3 == 2:
                            outputs(b, step[1] // 3, own)
                    elif step[0] == "nstat":
                        dve.wait_ge(s["xs_in"], 16 * (b + step[1] + 1))
                        for t in range(T):
                            last = dve.bn_stats(bn[:, 0, t, :], xs[:, t, :])
                        own_step(own, last)
                        for t in range(T):
                            last = dve.bn_aggr(mv[:, 0, t, :], bn[:, 0, t, :])
                        last.then_inc(s["stat"], 1)
                    elif step[0] in ("nnorm", "pnorm"):
                        which, rows, n, done = (0, xs, b + step[1] + 1, "z_ready") if step[0] == "nnorm" else (1, acc, b + 1, "out_ready")
                        stand(dve, s["rstd_ready" if which == 0 else "rstd2_ready"], n, s["stood"])
                        for t in range(T):
                            last = dve.tensor_scalar(rows[:, t, :], rows[:, t, :], mv[:, which, t, 0:1], rstd[:, which, t:t + 1],
                                                     ALU.subtract, ALU.mult)
                        last.then_inc(s[done], 1)
                    elif step[0] == "nz":
                        for j, (bank, _, _) in enumerate(uses):
                            dve.wait_ge(s["z_hi"], 2 * (b + 1) + j + 1)
                            dve.tensor_tensor(zl[:, 2 * j:2 * j + 2, :], F_ps[bank][:, :].rearrange("p (a q) -> p a q", a=2), fp(zh[:, 2 * j:2 * j + 2, :]),
                                              ALU.subtract).then_inc(s["f_dve"], 1)
                    elif step[0] == "nproj":
                        i = step[1]
                        bank, ready, _ = uses[0]
                        dve.wait_ge(s["f_ready"], ready)
                        dve.wait_ge(s["turned_ready"], 4 * (b + 1) + i + 1)
                        dve.tensor_tensor(biased[i % 2][:, :], F_ps[bank][:, :], bias[i % 2][:, :], ALU.add).then_inc(s["f_dve"], 1)
                    elif step[0] == "nstack":
                        turned_lo(b, step[1])
                    elif step[0] == "nval":
                        t = step[1]
                        bank, ready, _ = uses[0]
                        dve.wait_ge(s["f_ready"], ready)
                        dve.wait_ge(s["v_lo"], 2 * (b + 1) + t + 1)
                        dve.tensor_tensor(vfull[t][:, :], F_ps[bank][:, :], bias[2][:, :], ALU.add).then_inc(s["f_dve"], 1)
                    elif step[0] in ("split", "nsplit"):
                        t = step[1]
                        dve.wait_ge(s["v_hi"], 2 * (b + (step[0] == "nsplit")) + t + 1)
                        dve.tensor_tensor(v[t][:, :, 1, :], vfull[t][:, :].rearrange("p (h d) -> p h d", h=HEADS), fp(v[t][:, :, 0, :]),
                                          ALU.subtract).then_inc(s["v_lo"], 1)
                    elif step[0] == "pot":
                        t = step[1]
                        bank, _, _ = uses[0]
                        dve.wait_ge(s["ot_hi"], 2 * b + t + 1)
                        dve.tensor_tensor(oTl[t][:, :, :], F_ps[bank][:, :].rearrange("p (a q) -> p a q", a=KT), fp(oTh[t][:, :, :]), ALU.subtract).then_inc(s["f_dve"], 1)
                    elif step[0] == "py":
                        t = step[1]
                        bank, ready, _ = uses[0]
                        dve.wait_ge(s["base_ready"], b + 1)
                        dve.wait_ge(s["f_ready"], ready)
                        dve.scalar_tensor_tensor(acc[:, t, :], acc[:, t, :], 2.0, F_ps[bank][:, :], ALU.mult, ALU.add).then_inc(s["f_dve"], 1)
                    elif step[0] == "pstat":
                        dve.wait_ge(s["f_dve"], ring.made["dve"])
                        for t in range(T):
                            last = dve.bn_stats(bn[:, 1, t, :], acc[:, t, :])
                        own_step(own, last)
                        for t in range(T):
                            last = dve.bn_aggr(mv[:, 1, t, :], bn[:, 1, t, :])
                        last.then_inc(s["stat2"], 1)
                    elif step[0] == "nturn":
                        g, w = step[1:]
                        for t, (bank, ready, _) in enumerate(uses if w == 1 else []):
                            dve.wait_ge(s["f_ready"], ready)
                            dve.tensor_copy(stackT[w][:, 4 * g:4 * g + 4, t * P:(t + 1) * P], F_ps[bank][:, :]
                                            .rearrange("p (h q) -> p h q", h=4)).then_inc(s["f_dve"], 1)

            def turned_lo(b, i):
                w, t = i % 2, i // 2
                dve.wait_ge(s["turned_hi"], 4 * (b + 1) + i + 1)
                places = stack[w][t][:, :, 2:4, :] if w == 0 else stack[w][t][:, :, 1:4:2, :]
                dve.tensor_tensor(places, turned[i % 2][:, :].rearrange("p (h d) -> p h d", h=HEADS).unsqueeze(2).to_broadcast([P, HEADS, 2, D1]),
                                  fp(stack[w][t][:, :, 0:1, :]).to_broadcast([P, HEADS, 2, D1]), ALU.subtract).then_inc(s["turned_lo"], 1)

            body(-1, FIRST1, spare_first(), OwnSteps())
            per_body = 1 + 4 + 1
            with dve.Fori(0, B - 1) as b:
                body(b, ORDER1, spare(b), OwnSteps(2 + per_body * b))
            body(B - 1, LAST1, spare(B - 1), OwnSteps(2 + per_body * (B - 1)))
            body(B, FINISH1, spare_last(), OwnSteps(2 + per_body * (B - 1) + 5))

        @block.tensor
        def _(pe):
            pe.sem_inc(s["t_ready"], 2)
            pe.sem_inc(s["pv_done"], 2)

            def body(b, order, ring, first):
                u0 = NU1 * b
                split = {}
                for step in order:
                    n, by = spare_uses(step)
                    uses = [ring.next(by) for _ in range(n)]
                    if step[0] == "S":
                        u = step[1]
                        t, heads, g = UNITS1[u]
                        nj = P * (t + 1)
                        pe.wait_ge(s["exp_done"], u0 + u + 1)
                        if u == 0:
                            pe.wait_ge(s["f_act"], spare(b).made["act"])
                            pe.wait_ge(s["f_dve"], spare(b).made["dve"] - after(ORDER1, ("nturn", 3, 1)))
                        for j, h in enumerate(heads):
                            pe.matmul(S_ps[u % 2][:, j * nj:(j + 1) * nj], stackT[0][:, h, t * P:(t + 1) * P],
                                      stackT[1][:, h, 0:nj], start=j == 0, stop=False)
                        pe.matmul(S_ps[u % 2][:, :].rearrange("p (h j) -> p h j", j=nj)[:, :, nj - P:nj], identb[:, :],
                                  causal[:, :].unsqueeze(1).to_broadcast([P, len(heads), P]), start=False, stop=True).then_inc(s["s_ready"], 1)
                    elif step[0] == "T":
                        u = step[1]
                        pe.wait_ge(s["exp_done"], u0 + u + 3)
                        pe.wait_ge(s["p_lo"], u0 + u + 1)
                        for a in range(4):
                            last = pe.transpose(T_ps[u % 2][:, a * P:(a + 1) * P], probs[u % 2][:, a * P:(a + 1) * P], ident[:, :])
                        last.then_inc(s["t_ready"], 1)
                    elif step[0] == "V":
                        u = step[1]
                        t, heads, g = UNITS1[u]
                        pe.wait_ge(s["p_lo"], u0 + u + 3)
                        if u < T:
                            pe.wait_ge(s["v_lo"], 2 * b + u + 1 + 2)
                        if u % 3 == 0:
                            pe.wait_ge(s["o_ready"], 4 * b + g + 1)
                        for j, h in enumerate(heads):
                            to = O_ps[g % 2][:, (t * 4 + h % 4) * 2 * D1:(t * 4 + h % 4 + 1) * 2 * D1]
                            for a in range(t + 1):
                                pe.matmul(to, pTh[u % 2][:, j * (t + 1) + a, :], v[a][:, h, :, :], start=a == 0, stop=False)
                                last = pe.matmul(to[:, 0:D1], pTl[u % 2][:, j * (t + 1) + a, :], v[a][:, h, 0, :],
                                                 start=False, stop=a == t)
                        last.then_inc(s["pv_done"], 1)
                    elif step[0] == "nz":
                        pe.wait_ge(s["z_ready"], b + 2)
                        for j, (bank, _, before) in enumerate(uses):
                            wait_spare(pe, before, first)
                            for a in range(2):
                                for t in range(T):
                                    k = 2 * j + a
                                    last = pe.transpose(F_ps[bank][:, a * L + t * P:a * L + (t + 1) * P],
                                                        xs[:, t, k * P:(k + 1) * P], ident[:, :])
                            last.then_inc(s["f_ready"], 1)
                    elif step[0] == "nproj" or step[0] == "nval":
                        i = step[1]
                        w, t = (i % 2, i // 2) if step[0] == "nproj" else (2, i)
                        bank, _, before = uses[0]
                        wait_spare(pe, before, first)
                        if step == ("nproj", 0):
                            pe.wait_ge(s["f_dve"], ring.made["dve"] - 1)
                        for k in range(KT):
                            last = product3(pe, F_ps[bank][:, :], (zh[:, k, t * P:(t + 1) * P], zl[:, k, t * P:(t + 1) * P]),
                                            (wh[w][:, k, :], wl[w][:, k, :]), k == 0, k == KT - 1)
                        last.then_inc(s["f_ready"], 1)
                    elif step[0] == "nturn":
                        g, w = step[1:]
                        if (g, w) == (0, 0):
                            pe.wait_ge(s["turned_lo"], 4 * (b + 2) + 2)
                        for t, (bank, _, before) in enumerate(uses):
                            wait_spare(pe, before, first)
                            for a in range(4):
                                last = pe.transpose(F_ps[bank][:, a * P:(a + 1) * P], fp(stack[w][t][:, 4 * g + a, :, :]), ident[:, :])
                            last.then_inc(s["f_ready"], 1)
                    elif step[0] == "pot":
                        t = step[1]
                        bank, _, before = uses[0]
                        split[t] = ring.made["dve"]
                        wait_spare(pe, before, first)
                        pe.wait_ge(s["o_ready"], 4 * b + 2)
                        for k in range(KT):
                            last = pe.transpose(F_ps[bank][:, k * P:(k + 1) * P], o[:, t, k * P:(k + 1) * P], ident[:, :])
                        last.then_inc(s["f_ready"], 1)
                    elif step[0] == "py":
                        t = step[1]
                        bank, _, before = uses[0]
                        wait_spare(pe, before, first)
                        pe.wait_ge(s["f_dve"], split[t])
                        for k in range(KT):
                            last = product3(pe, F_ps[bank][:, :], (oTh[t][:, k, :], oTl[t][:, k, :]),
                                            (wh[3][:, k, :], wl[3][:, k, :]), k == 0, k == KT - 1)
                        last.then_inc(s["f_ready"], 1)

            body(-1, FIRST1, spare_first(), True)
            with pe.Fori(0, B - 1) as b:
                body(b, ORDER1, spare(b), False)
            body(B - 1, LAST1, spare(B - 1), False)
            body(B, FINISH1, spare_last(), False)



D2 = 64
EMBED = HEADS * D2
PAIRS = HEADS // 2
WINDOW = 128

ORDER2 = [("S", 0), ("norm", 0), ("prj", 1), ("S", 1), ("T", 0), ("S", 2), ("T", 1), ("prj", 2), ("xt", 0), ("S", 3), ("V", 0),
          ("V", 1), ("T", 2), ("S", 4), ("T", 3), ("prj", 3), ("xt", 1), ("V", 2), ("ot", 0), ("S", 5), ("T", 4), ("V", 3),
          ("S", 6), ("T", 5), ("prj", 4), ("y", 0), ("ot", 1), ("V", 4), ("T", 6), ("S", 7), ("V", 5), ("S", 8), ("y", 1),
          ("T", 7), ("prj", 5), ("V", 6), ("ot", 2), ("S", 9), ("V", 7), ("T", 8), ("y", 2), ("T", 9), ("S", 10), ("prj", 6),
          ("ot", 3), ("V", 8), ("S", 11), ("T", 10), ("y", 3), ("S", 12), ("V", 9), ("T", 11), ("prj", 7), ("V", 10),
          ("ot", 4), ("S", 13), ("V", 11), ("T", 12), ("y", 4), ("S", 14), ("T", 13), ("V", 12), ("ot", 5), ("nx", 0),
          ("S", 15), ("T", 14), ("nx", 1), ("V", 13), ("nx", 2), ("y", 5), ("T", 15), ("nx", 3), ("ot", 6), ("V", 14),
          ("V", 15), ("nprj", 0), ("nv", 0), ("y", 6), ("ot", 7), ("nv", 1), ("nv", 2), ("y", 7), ("nv", 3)]
FIRST2 = [("nx", j) for j in range(4)] + [("nprj", 0), ("nv", 0), ("nv", 1), ("nv", 2), ("nv", 3)]
LAST2 = [st for st in ORDER2 if st[0] not in ("nx", "nprj", "nv")] + [("lnorm", 0), ("lxt", 0), ("lxt", 1)]


def score_uses(kind):
    return {"S": (1, "act"), "xt": (1, "dve"), "lxt": (1, "dve"), "nx": (1, "dve"), "nv": (1, "dve")}.get(kind, (0, "dve"))


def cross_attention(nc, x1, context, weights, x2, x2T, pooled_out, raw, w_in):
    with ExitStack() as ctx:
        def sb(name, shape, dt=F32):
            return ctx.enter_context(nc.sbuf_tensor(name, shape, dt))

        def sem(name):
            return ctx.enter_context(nc.semaphore(name))

        def banks(name, n):
            return [ctx.enter_context(nc.psum_tensor(f"{name}{i}", [P, 512], F32)) for i in range(n)]

        xs = sb("c_xs", [P, 2, T, D])
        inTh = sb("c_inTh", [P, 2, KT, L], F32R)
        inTl = sb("c_inTl", [P, 2, KT, L], F32R)
        v = [sb(f"c_v{t}", [P, HEADS, 2, D2], F32R) for t in range(T)]
        outT = sb("c_outT", [P, KT, L])
        probs = [sb(f"c_probs{i}", [P, 2, L]) for i in range(2)]

        rows = [KT, KT, KT, PAIRS]
        cols = [EMBED, EMBED, EMBED, D]
        wh = [sb(f"c_wh{i}", [P, rows[i], cols[i]], F32R) for i in range(4)]
        wl = [sb(f"c_wl{i}", [P, rows[i], cols[i]], F32R) for i in range(4)]
        ident = sb("c_ident", [P, P])
        identb = sb("c_identb", [P, P], BF16)
        far = [sb(f"c_far{t}", [P, P], BF16) for t in range(T)]
        half = sb("c_half", [P, T])
        pooled = sb("c_pooled", [P, KT, B + 1])
        qh = [sb(f"c_qh{i}", [P, 2, L], F32R) for i in range(2)]
        ql = [sb(f"c_ql{i}", [P, 2, L], F32R) for i in range(2)]
        kh = [sb(f"c_kh{i}", [P, L], F32R) for i in range(2)]
        kl = [sb(f"c_kl{i}", [P, L], F32R) for i in range(2)]
        acc = sb("c_acc", [P, T, D])
        mv = sb("c_mv", [P, T, 2])
        rstd = sb("c_rstd", [P, T])

        S_ps, T_ps, F_ps, O_ps, Y_ps = banks("c_S", 2), banks("c_T", 2), banks("c_F", 1)[0], banks("c_O", 1)[0], banks("c_Y", 2)

        names = ["xs_in", "acc_in", "out_done", "outT_done", "pooled_done", "s_ready", "s_dve", "exp_done", "max_ready", "n_hi",
                 "t_ready", "t_hi", "t_dve", "f_ready", "f_hi", "f_dve", "pv_done", "o_ready", "y_ready", "y_dve",
                 "stat", "rstd_ready", "out_ready", "outT_ready", "own_dve", "own_pool", "stood"]
        s = {n: sem("c_" + n) for n in names}

        def rows_of(tensor, b):
            return tensor[b].rearrange("(t p) d -> p t d", p=P)

        def load_inputs(sp, b):
            sp.dma_start(xs[:, 0, :, :], rows_of(x1, b + 1)).then_inc(s["xs_in"], 16)
            sp.dma_start(xs[:, 1, :, :], rows_of(context, b)).then_inc(s["xs_in"], 16)

        with ExitStack() as sctx:
            raw_o = sctx.enter_context(nc.sbuf_tensor("c_raw_o", [P, PAIRS // 2, D], F32))
            pieces = [(i, slice(0, KT), raw[:, i, :].rearrange("p (t n) -> p t n", t=KT)) for i in range(3)]
            pieces += [(3, slice(0, PAIRS // 2), raw_o[:, :, :]),
                       (3, slice(PAIRS // 2, PAIRS), raw[:, 0, PAIRS // 2 * D:].rearrange("p (t n) -> p t n", n=D))]
            made = sctx.enter_context(nc.semaphore("c_made"))
            w_hi = sctx.enter_context(nc.semaphore("c_w_hi"))
            w_lo = sctx.enter_context(nc.semaphore("c_w_lo"))
            block = sctx.enter_context(nc.Block())

            def low(eng, n):
                i, tiles, where = pieces[n]
                eng.wait_ge(w_hi, n + 1)
                return eng.tensor_tensor(wl[i][:, tiles, :], where, fp(wh[i][:, tiles, :]), ALU.subtract)

            @block.sync
            def _(sp):
                def load_wo(n):
                    _, tiles, where = pieces[n]
                    sp.dma_start(where, weights[3].rearrange("(t p) n -> p t n", p=P)[:, tiles, :]).then_inc(w_in[n], 16)

                load_wo(3)
                sp.wait_ge(w_lo, 1)
                load_wo(4)
                load_inputs(sp, 0)

            @block.gpsimd
            def _(pool):
                for m in (ident, identb, far[0], far[1]):
                    last = pool.memset(m[:, :], 0.0)
                last.then_inc(made, 1)
                pool.memset(half[:, :], -0.5)
                for m in (acc[:, :, :], mv[:, :, :], rstd[:, :]):
                    pool.memset(m, 0.0)
                for i in range(2):
                    pool.memset(fp(qh[i][:, :, :]), 0.0)
                    pool.memset(fp(ql[i][:, :, :]), 0.0)
                pool.wait_ge(made, 1)
                for m in (ident, identb):
                    pool.affine_select(m[:, :], m[:, :], [[-1, P]], ALU.not_equal, 1.0, base=0, channel_multiplier=1)
                pool.affine_select(far[0][:, :], far[0][:, :], [[-1, P]], ALU.is_ge, MASKED, base=0, channel_multiplier=1)
                pool.affine_select(far[1][:, :], far[1][:, :], [[1, P]], ALU.is_ge, MASKED, base=0, channel_multiplier=-1)

                pool.wait_ge(w_in[1], 16)
                low(pool, 1)

            @block.vector
            def _(dve):
                for n in (0, 2, 3, 4):
                    dve.wait_ge(w_in[n], 16)
                    low(dve, n).then_inc(w_lo, 1)

            @block.scalar
            def _(act):
                for n, (i, tiles, where) in enumerate(pieces):
                    act.wait_ge(w_in[n], 16)
                    act.activation(wh[i][:, tiles, :], where, ACT.Copy).then_inc(w_hi, 1)

        negmax = sb("c_negmax", [P, 2, 2])
        sums = sb("c_sums", [P, T, HEADS])
        pTh = [sb(f"c_pTh{i}", [P, 4, P], F32R) for i in range(2)]
        pTl = [sb(f"c_pTl{i}", [P, 4, P], F32R) for i in range(2)]
        rsum = sb("c_rsum", [P, T, 2])
        o = sb("c_o", [P, T, 2, D2])
        oTh = [sb(f"c_oTh{i}", [P, L], F32R) for i in range(2)]
        oTl = [sb(f"c_oTl{i}", [P, L], F32R) for i in range(2)]
        bn = sb("c_bn", [P, T, 6])
        ve = sb("c_ve", [P, T])

        block = ctx.enter_context(nc.Block())

        def score_banks(b):
            return SpareBanks(8 + 26 * b, 8 + 10 * b, 2 + 16 * b)

        def turn_banks(b):
            return SpareBanks(24 * b, 24 * b + 2, 0)


        def turn_uses(kind):
            return 1 if kind in ("T", "ot") else 0

        def project_count(b, kind, m):
            return PAIRS * (b + (kind == "nprj")) + m + 1

        @block.sync
        def _(sp):
            sp.sem_inc(s["outT_done"], 16)

            def batch(b, more):
                if more:
                    sp.wait_ge(s["s_ready"], 4 if isinstance(b, int) else 8 + 26 * (b - 1) + to_nx)
                    load_inputs(sp, b + 1)
                store(b - 1)
                store_transposed(b)
                sp.wait_ge(s["out_done"], 16 * (b + 1))
                sp.dma_start(acc[:, :, :], rows_of(x1, b + 1)).then_inc(s["acc_in"], 16)

            def store(b):
                sp.wait_ge(s["out_ready"], b + 2)
                sp.dma_start(rows_of(x2, b + 1), acc[:, :, :]).then_inc(s["out_done"], 16)

            def store_transposed(b):
                sp.wait_ge(s["outT_ready"], 2 * b + 2)
                sp.dma_start(x2T[b], outT[:, :, :]).then_inc(s["outT_done"], 16)

            to_nx = sum(score_uses(kind)[0] for kind, _ in ORDER2[:ORDER2.index(("nx", 3)) + 1])
            batch(0, True)
            with sp.Fori(1, B - 1) as b:
                batch(b, True)
            batch(B - 1, False)
            store(B - 1)
            store_transposed(B)
            sp.wait_ge(s["s_dve"], 8 + 10 * (B - 1) + 4)
            sp.dma_start(pooled_out, pooled[:, :, :]).then_inc(s["pooled_done"], 16)
            sp.wait_ge(s["pooled_done"], 16)
            sp.wait_ge(s["out_done"], 16 * (B + 1))
            sp.wait_ge(s["outT_done"], 16 * (B + 2))

        @block.gpsimd
        def _(pool):
            pool.sem_inc(s["rstd_ready"], 1)
            with pool.Fori(0, B) as b:
                stand(pool, s["stat"], b + 1, s["stood"])
                pool.tensor_scalar(ve[:, :], mv[:, :, 1], EPS, None, ALU.add).then_inc(s["own_pool"], 1)
                pool.wait_ge(s["own_pool"], b + 1)
                pool.tensor_tensor(rstd[:, :], ve[:, :], half[:, :], ALU.pow).then_inc(s["rstd_ready"], 1)

        @block.scalar
        def _(act):
            act.sem_inc(s["exp_done"], 2)

            def body(b, order, ring, turns, first):
                for kind, i in order:
                    n, by = score_uses(kind)
                    uses = [ring.next(by) for _ in range(n)]
                    uses += [turns.next("dve") for _ in range(turn_uses(kind))]
                    if kind == "S":
                        act.wait_ge(s["max_ready"], 16 * b + i + 1)
                        for j in range(2):
                            last = act.activation(probs[i % 2][:, j, :], S_ps[uses[0][0]][:, j * L:(j + 1) * L], ACT.Exp,
                                                  bias=negmax[:, i % 2, j:j + 1], accum_out=sums[:, i % 2, i - i % 2 + j:i - i % 2 + j + 1])
                        last.then_inc(s["exp_done"], 1)
                    elif kind in ("T", "ot"):
                        bank, ready, _ = uses[0]
                        act.wait_ge(s["t_ready"], ready)
                        to, n = (pTh[i % 2][:, :, :], 512) if kind == "T" else (oTh[i % 2][:, :], L)
                        act.activation(to, T_ps[bank][:, 0:n], ACT.Copy).then_inc(s["t_hi"], 1)
                    elif kind in ("prj", "nprj"):
                        act.wait_ge(s["f_ready"], project_count(b, kind, i))
                        for j in range(2):
                            h = slice(j * D2, (j + 1) * D2)
                            act.activation(qh[i % 2][h, j, :], F_ps[h, 0:L], ACT.Copy, scale=D2 ** -0.5)
                        act.activation(kh[i % 2][:, :], F_ps[:, L:2 * L], ACT.Copy).then_inc(s["f_hi"], 1)
                    elif kind == "nx":
                        bank, ready, _ = uses[0]
                        act.wait_ge(s["s_ready"], ready)
                        act.activation(inTh[:, i // 2, 2 * (i % 2):2 * (i % 2) + 2, :], S_ps[bank][:, :], ACT.Copy).then_inc(s["n_hi"], 1)
                    elif kind == "nv":
                        bank, ready, _ = uses[0]
                        act.wait_ge(s["s_ready"], ready)
                        if not first:
                            act.wait_ge(s["pv_done"], PAIRS * (b + 1))
                        act.activation(v[i // 2][:, 8 * (i % 2):8 * (i % 2) + 8, 0, :], S_ps[bank][:, :]
                                       .rearrange("p (h d) -> p h d", h=8), ACT.Copy).then_inc(s["n_hi"], 1)
                    elif kind in ("xt", "lxt"):
                        bank, ready, _ = uses[0]
                        act.wait_ge(s["outT_done"], 16 * (b + (kind == "lxt") + 1))
                        act.wait_ge(s["s_ready"], ready)
                        act.activation(outT[:, 2 * i:2 * i + 2, :], S_ps[bank][:, :], ACT.Copy).then_inc(s["outT_ready"], 1)

            body(-1, FIRST2, SpareBanks(0, 0, 0), turn_banks(0), True)
            with act.Fori(0, B - 1) as b:
                body(b, ORDER2, score_banks(b), turn_banks(b), False)
            body(B - 1, LAST2, score_banks(B - 1), turn_banks(B - 1), False)

        @block.vector
        def _(dve):
            dve.sem_inc(s["t_dve"], 2)
            dve.sem_inc(s["f_dve"], 1)
            dve.sem_inc(s["o_ready"], 1)
            dve.sem_inc(s["y_dve"], 1)

            def outputs(b, m, own):
                dve.wait_ge(s["pv_done"], PAIRS * b + m + 1)
                dve.wait_ge(s["o_ready"], PAIRS * b + m + 1)
                dve.reciprocal(rsum[:, :, :], sums[:, :, 2 * m:2 * m + 2])
                dve.tensor_reduce(o[:, :, :, :].rearrange("p t h d -> p (t h) d"), O_ps[:, :]
                                  .rearrange("p (g e d) -> p g d e", e=2, d=D2), AX.X, ALU.add).then_inc(s["own_dve"], 1)
                stand(dve, s["own_dve"], own.next(), s["stood"])
                dve.tensor_tensor(o[:, :, :, :], o[:, :, :, :], rsum[:, :, :].unsqueeze(3).to_broadcast([P, T, 2, D2]),
                                  ALU.mult).then_inc(s["o_ready"], 1)

            def body(b, order, ring, turns, own):
                for kind, i in order:
                    n, by = score_uses(kind)
                    uses = [ring.next(by) for _ in range(n)]
                    uses += [turns.next("dve") for _ in range(turn_uses(kind))]
                    if kind == "S":
                        bank, ready, _ = uses[0]
                        dve.wait_ge(s["s_ready"], ready)
                        dve.wait_ge(s["exp_done"], 16 * b + i + 1)
                        dve.tensor_reduce(negmax[:, i % 2, :], S_ps[bank][:, :].rearrange("p (h j) -> p h j", h=2),
                                          AX.X, ALU.max, negate=True).then_inc(s["max_ready"], 1)
                    elif kind in ("T", "ot"):
                        bank, ready, _ = uses[0]
                        dve.wait_ge(s["t_hi"], ready)
                        if kind == "T":
                            dve.tensor_tensor(pTl[i % 2][:, :, :], T_ps[bank][:, :].rearrange("p (a q) -> p a q", a=4),
                                              fp(pTh[i % 2][:, :, :]), ALU.subtract).then_inc(s["t_dve"], 1)
                        else:
                            dve.tensor_tensor(oTl[i % 2][:, :], T_ps[bank][:, 0:L], fp(oTh[i % 2][:, :]), ALU.subtract).then_inc(s["t_dve"], 1)
                    elif kind == "V":
                        if i % 2 == 1:
                            outputs(b, i // 2, own)
                    elif kind in ("prj", "nprj"):
                        dve.wait_ge(s["f_hi"], project_count(b, kind, i))
                        for j in range(2):
                            h = slice(j * D2, (j + 1) * D2)
                            dve.scalar_tensor_tensor(ql[i % 2][h, j, :], F_ps[h, 0:L], D2 ** -0.5, fp(qh[i % 2][h, j, :]),
                                                     ALU.mult, ALU.subtract)
                        dve.tensor_tensor(kl[i % 2][:, :], F_ps[:, L:2 * L], fp(kh[i % 2][:, :]), ALU.subtract).then_inc(s["f_dve"], 1)
                    elif kind == "nx":
                        bank, _, _ = uses[0]
                        half_of = (slice(None), i // 2, slice(2 * (i % 2), 2 * (i % 2) + 2))
                        dve.wait_ge(s["n_hi"], 8 * (b + 1) + i + 1)
                        dve.tensor_tensor(inTl[half_of], S_ps[bank][:, :].rearrange("p (a q) -> p a q", a=2), fp(inTh[half_of]),
                                          ALU.subtract).then_inc(s["s_dve"], 1)
                    elif kind == "nv":
                        bank, _, _ = uses[0]
                        dve.wait_ge(s["n_hi"], 8 * (b + 1) + 4 + i + 1)
                        h = slice(8 * (i % 2), 8 * (i % 2) + 8)
                        dve.tensor_tensor(v[i // 2][:, h, 1, :], S_ps[bank][:, :].rearrange("p (h d) -> p h d", h=8),
                                          fp(v[i // 2][:, h, 0, :]), ALU.subtract).then_inc(s["s_dve"], 1)
                    elif kind in ("xt", "lxt"):
                        bank, _, _ = uses[0]
                        entry = b + (kind == "lxt")
                        dve.wait_ge(s["outT_ready"], 2 * entry + i + 1)
                        dve.tensor_reduce(pooled[:, 2 * i:2 * i + 2, entry], S_ps[bank][:, :].rearrange("p (a q) -> p a q", a=2),
                                          AX.X, ALU.add).then_inc(s["s_dve"], 1)
                    elif kind in ("norm", "lnorm"):
                        stand(dve, s["rstd_ready"], b + (kind == "lnorm") + 1, s["stood"])
                        for t in range(T):
                            last = dve.tensor_scalar(acc[:, t, :], acc[:, t, :], mv[:, t, 0:1], rstd[:, t:t + 1], ALU.subtract, ALU.mult)
                        last.then_inc(s["out_ready"], 1)
                    elif (kind, i) == ("y", PAIRS - 1):
                        dve.wait_ge(s["acc_in"], 16 * (b + 1))
                        dve.wait_ge(s["y_ready"], b + 1)
                        for t in range(T):
                            last = dve.tensor_tensor(acc[:, t, :], Y_ps[t][:, :], acc[:, t, :], ALU.add)
                        last.then_inc(s["y_dve"], 1)
                        dve.wait_ge(s["y_dve"], b + 2)
                        for t in range(T):
                            last = dve.bn_stats(bn[:, t, :], acc[:, t, :])
                        last.then_inc(s["own_dve"], 1)
                        stand(dve, s["own_dve"], own.next(), s["stood"])
                        for t in range(T):
                            last = dve.bn_aggr(mv[:, t, :], bn[:, t, :])
                        last.then_inc(s["stat"], 1)

            body(-1, FIRST2, SpareBanks(0, 0, 0), turn_banks(0), OwnSteps())
            per_body = PAIRS + 1
            with dve.Fori(0, B - 1) as b:
                body(b, ORDER2, score_banks(b), turn_banks(b), OwnSteps(per_body * b))
            body(B - 1, LAST2, score_banks(B - 1), turn_banks(B - 1), OwnSteps(per_body * (B - 1)))

        @block.tensor
        def _(pe):
            def wait_score_bank(before, first):
                by, count = before
                if not (first and count <= 0):
                    pe.wait_ge(s["exp_done" if by == "act" else "s_dve"], count)

            def body(b, order, ring, turns, first):
                turned = {}
                for kind, i in order:
                    n, by = score_uses(kind)
                    uses = [ring.next(by) for _ in range(n)]
                    if turn_uses(kind):
                        bank, ready, before = turns.next("dve")
                        turned[kind, i] = turns.made["dve"]
                        pe.wait_ge(s["t_dve"], before[1])
                    if kind == "S":
                        bank, _, before = uses[0]
                        t, m = i % 2, i // 2
                        wait_score_bank(before, first)
                        if t == 0:
                            pe.wait_ge(s["f_dve"], project_count(b, kind, m) + 1)
                        q = slice(t * P, (t + 1) * P)
                        for j in range(2):
                            product3(pe, S_ps[bank][:, j * L:(j + 1) * L], (qh[m % 2][:, j, q], ql[m % 2][:, j, q]),
                                     (kh[m % 2][:, :], kl[m % 2][:, :]), j == 0, False)
                        last = pe.matmul(S_ps[bank][:, :].rearrange("p (j l) -> p j l", j=2)[:, :, (1 - t) * P:(2 - t) * P], identb[:, :],
                                         far[t][:, :].unsqueeze(1).to_broadcast([P, 2, P]), start=False, stop=True)
                        last.then_inc(s["s_ready"], 1)
                    elif kind == "T":
                        pe.wait_ge(s["exp_done"], 16 * b + i + 3)
                        for a in range(4):
                            last = pe.transpose(T_ps[bank][:, a * P:(a + 1) * P], probs[i % 2][:, a // 2, (a % 2) * P:(a % 2 + 1) * P], ident[:, :])
                        last.then_inc(s["t_ready"], 1)
                    elif kind == "V":
                        t, m = i % 2, i // 2
                        pe.wait_ge(s["t_dve"], turned["T", i])
                        if i == 0:
                            pe.wait_ge(s["s_dve"], 8 + 10 * b)
                        if t == 0:
                            pe.wait_ge(s["o_ready"], PAIRS * b + m + 1)
                        for j in range(2):
                            to = O_ps[:, (t * 2 + j) * 2 * D2:(t * 2 + j + 1) * 2 * D2]
                            for a in range(T):
                                pe.matmul(to, pTh[i % 2][:, j * 2 + a, :], v[a][:, 2 * m + j, :, :], start=a == 0, stop=False)
                                last = pe.matmul(to[:, 0:D2], pTl[i % 2][:, j * 2 + a, :], v[a][:, 2 * m + j, 0, :], start=False, stop=a == 1)
                        if t == 1:
                            last.then_inc(s["pv_done"], 1)
                    elif kind in ("prj", "nprj"):
                        if kind == "nprj":
                            pe.wait_ge(s["s_dve"], ring.made["dve"])
                        pe.wait_ge(s["f_dve"], project_count(b, kind, i))
                        for w in range(2):
                            for k in range(KT):
                                last = product3(pe, F_ps[:, w * L:(w + 1) * L], (wh[w][:, k, i * P:(i + 1) * P], wl[w][:, k, i * P:(i + 1) * P]),
                                                (inTh[:, w, k, :], inTl[:, w, k, :]), k == 0, k == KT - 1)
                        last.then_inc(s["f_ready"], 1)
                    elif kind == "ot":
                        pe.wait_ge(s["o_ready"], PAIRS * b + i + 2)
                        for t in range(T):
                            last = pe.transpose(T_ps[bank][:, t * P:(t + 1) * P], o[:, t, :, :], ident[:, :])
                        last.then_inc(s["t_ready"], 1)
                    elif kind == "y":
                        pe.wait_ge(s["t_dve"], turned["ot", i])
                        if i == 0:
                            pe.wait_ge(s["y_dve"], b + 1)
                        for t in range(T):
                            q = slice(t * P, (t + 1) * P)
                            last = product3(pe, Y_ps[t][:, :], (oTh[i % 2][:, q], oTl[i % 2][:, q]), (wh[3][:, i, :], wl[3][:, i, :]),
                                            i == 0, i == PAIRS - 1)
                        if i == PAIRS - 1:
                            last.then_inc(s["y_ready"], 1)
                    elif kind == "nx":
                        pe.wait_ge(s["xs_in"], 32 * (b + 2))
                        bank, _, before = uses[0]
                        wait_score_bank(before, first)
                        for a in range(2):
                            for t in range(T):
                                k = 2 * (i % 2) + a
                                last = pe.transpose(S_ps[bank][:, a * L + t * P:a * L + (t + 1) * P], xs[:, i // 2, t, k * P:(k + 1) * P], ident[:, :])
                        last.then_inc(s["s_ready"], 1)
                    elif kind == "nv":
                        bank, _, before = uses[0]
                        wait_score_bank(before, first)
                        t, c = i // 2, slice((i % 2) * 512, (i % 2 + 1) * 512)
                        if i == 0:
                            pe.wait_ge(s["s_dve"], ring.made["dve"] - 1)
                        for k in range(KT):
                            last = product3(pe, S_ps[bank][:, :], (inTh[:, 1, k, t * P:(t + 1) * P], inTl[:, 1, k, t * P:(t + 1) * P]),
                                            (wh[2][:, k, c], wl[2][:, k, c]), k == 0, k == KT - 1)
                        last.then_inc(s["s_ready"], 1)
                    elif kind in ("xt", "lxt"):
                        bank, _, before = uses[0]
                        pe.wait_ge(s["out_ready"], b + (kind == "lxt") + 1)
                        wait_score_bank(before, first)
                        for a in range(2):
                            for t in range(T):
                                k = 2 * i + a
                                last = pe.transpose(S_ps[bank][:, a * L + t * P:a * L + (t + 1) * P], acc[:, t, k * P:(k + 1) * P], ident[:, :])
                        last.then_inc(s["s_ready"], 1)

            body(-1, FIRST2, SpareBanks(0, 0, 0), turn_banks(0), True)
            with pe.Fori(0, B - 1) as b:
                body(b, ORDER2, score_banks(b), turn_banks(b), False)
            body(B - 1, LAST2, score_banks(B - 1), turn_banks(B - 1), False)



FC = 4
FT = FF // P // FC
RING = 4

CHUNKS = [("w1", 0), ("w1", 1), ("w2", 0), ("w1", 2), ("w2", 1), ("w1", 3), ("w2", 2), ("w2", 3)]
LATE = CHUNKS[-1]
ORDER3 = [("h", 1), ("nsplit", ("w1", 0)), ("nsplit", ("w1", 1)), ("y", 0), ("nsplit", ("w2", 0)),
          ("h", 2), ("nsplit", ("w1", 2)), ("base", 0), ("y", 1), ("nsplit", ("w2", 1)), ("h", 3), ("nsplit", ("w1", 3)),
          ("nx", 0), ("y", 2), ("nsplit", ("w2", 2)), ("nh", 0), ("y", 3), ("end", 0)]
FIRST3 = [("nx", 0)] + [("nsplit", c) for c in CHUNKS[:2]] + [("nh", 0)] + [("nsplit", c) for c in CHUNKS[2:-1]]
LAST3 = [st for st in ORDER3 if st[0][0] != "n"]


def route(nc, pooled_in, wr, banks, table, etab, btab, newtab):
    with ExitStack() as ctx:
        def sb(name, shape, dt=F32):
            return ctx.enter_context(nc.sbuf_tensor("r_" + name, shape, dt))

        pooled = sb("pooled", [P, KT, B + 1])
        wrs = sb("wr", [P, KT, E])
        logits, top = sb("logits", [B, E]), sb("top", [B, 8])
        index = sb("index", [B, 8], mybir.dt.uint32)
        gap, second, total = sb("gap", [B, 1]), sb("second", [B, 1]), sb("total", [B, 1])
        iota_k, iota_s, iota_b = sb("iota_k", [B, 2], I32), sb("iota_s", [B, SLOTS], I32), sb("iota_b", [B, 1], I32)
        pair_no, slot_no = sb("pair_no", [B, 2]), sb("slot_no", [B, SLOTS])
        value = sb("value", [B, 2, 3])
        key = sb("key", [B, 2])
        ident, ones = sb("ident", [B, B]), sb("ones", [B, B])
        spread = sb("spread", [B, B, 2])
        less = sb("less", [B, 2, SLOTS])
        rank = sb("rank", [B, 2])
        chosen = sb("chosen", [B, 2, SLOTS])
        wide = sb("wide", [B, 2, 3, P])
        ps, pk, pt = banks[0:3]
        s = {n: ctx.enter_context(nc.semaphore("r_" + n)) for n in
             ["loaded", "made", "logits_ready", "gap_ready", "second_ready", "spread_ready", "keys_ready", "wide_ready", "table_ready", "own"]}
        block = ctx.enter_context(nc.Block())

        @block.sync
        def _(sp):
            sp.dma_start(pooled[:, :, :], pooled_in).then_inc(s["loaded"], 16)
            sp.dma_start(wrs[:, :, :], wr.rearrange("(t p) e -> p t e", p=P)).then_inc(s["loaded"], 16)

        @block.gpsimd
        def _(pool):
            pool.memset(ident[:, :], 0.0).then_inc(s["made"], 1)
            pool.memset(ones[:, :], 1.0)
            pool.iota(iota_k[:, :], [[1, 2]], base=0, channel_multiplier=2)
            pool.iota(iota_s[:, :], [[1, SLOTS]], base=0, channel_multiplier=0)
            pool.iota(iota_b[:, :], [[1, 1]], base=0, channel_multiplier=1)
            pool.wait_ge(s["made"], 1)
            pool.affine_select(ident[:, :], ident[:, :], [[-1, B]], ALU.not_equal, 1.0, base=0, channel_multiplier=1).then_inc(s["made"], 1)

        @block.scalar
        def _(act):
            act.wait_ge(s["gap_ready"], 1)
            act.activation(second[:, :], gap[:, :], ACT.Exp).then_inc(s["second_ready"], 1)

        @block.tensor
        def _(pe):
            pe.wait_ge(s["loaded"], 32)
            for k in range(KT):
                last = pe.matmul(ps[0:B, 0:E], pooled[:, k, 1:B + 1], wrs[:, k, :], start=k == 0, stop=k == KT - 1)
            last.then_inc(s["logits_ready"], 1)
            pe.wait_ge(s["spread_ready"], 1)
            pe.matmul(pk[0:B, 0:SLOTS], ones[:, :], spread[:, :, :], start=True, stop=True).then_inc(s["keys_ready"], 1)
            pe.wait_ge(s["wide_ready"], 1)
            for c in range(3):
                for k in range(2):
                    last = pe.matmul(pt[:, c * SLOTS:(c + 1) * SLOTS], wide[:, k, c, :], chosen[:, k, :], start=k == 0, stop=k == 1)
            last.then_inc(s["table_ready"], 1)

        @block.vector
        def _(dve):
            done = [0]

            def own(instruction):
                done[0] += 1
                instruction.then_inc(s["own"], 1)
                dve.wait_ge(s["own"], done[0])

            dve.wait_ge(s["made"], 2)
            dve.tensor_copy(pair_no[:, :], iota_k[:, :])
            dve.tensor_copy(slot_no[:, :], iota_s[:, :])
            dve.tensor_copy(value[:, :, 1], iota_b[:, :].to_broadcast([B, 2]))
            dve.wait_ge(s["logits_ready"], 1)
            own(dve.tensor_scalar(logits[:, :], ps[0:B, 0:E], 1.0 / L, None, ALU.mult))
            own(dve.max(top[:, :], logits[:, :]))
            dve.max_index(index[:, :], top[:, :], logits[:, :])
            dve.tensor_tensor(gap[:, :], top[:, 1:2], top[:, 0:1], ALU.subtract).then_inc(s["gap_ready"], 1)
            dve.wait_ge(s["gap_ready"], 1)
            own(dve.tensor_copy(value[:, :, 0], index[:, 0:2]))
            own(dve.scalar_tensor_tensor(key[:, :], value[:, :, 0], float(SLOTS), pair_no[:, :], ALU.mult, ALU.add))
            for k in range(2):
                last = dve.tensor_scalar(spread[:, :, k], ident[:, :], key[:, k:k + 1], None, ALU.mult)
            last.then_inc(s["spread_ready"], 1)
            dve.wait_ge(s["second_ready"], 1)
            own(dve.tensor_scalar(total[:, :], second[:, :], 1.0, None, ALU.add))
            own(dve.reciprocal(value[:, 0, 2:3], total[:, :]))
            dve.tensor_tensor(value[:, 1, 2:3], second[:, :], value[:, 0, 2:3], ALU.mult)
            dve.wait_ge(s["keys_ready"], 1)
            for k in range(2):
                last = dve.tensor_scalar(less[:, k, :], pk[0:B, 0:SLOTS], key[:, k:k + 1], None, ALU.is_lt)
            own(last)
            own(dve.tensor_reduce(rank[:, :], less[:, :, :], AX.X, ALU.add))
            for k in range(2):
                dve.tensor_scalar(chosen[:, k, :], slot_no[:, :], rank[:, k:k + 1], None, ALU.is_equal)
            dve.tensor_copy(wide[:, :, :, :].rearrange("b k c p -> b (k c) p"), value[:, :, :].rearrange("b k c -> b (k c)")
                            .unsqueeze(2).to_broadcast([B, 6, P])).then_inc(s["wide_ready"], 1)
            dve.wait_ge(s["table_ready"], 1)
            own(dve.tensor_copy(table[:, :, :], pt[:, 0:3 * SLOTS].rearrange("p (c s) -> p c s", c=3)))
            dve.tensor_tensor(newtab[:, 1:SLOTS], table[0:1, 0, 1:SLOTS], table[0:1, 0, 0:SLOTS - 1], ALU.not_equal)
            dve.tensor_copy(etab[:, :], pt[0:1, 0:SLOTS])
            dve.tensor_copy(btab[:, :], pt[0:1, SLOTS:2 * SLOTS])


def experts(nc, x2, x2T, pooled_in, wr, w1, b1, w2, b2, out):
    with ExitStack() as ctx:
        def sb(name, shape, dt=F32):
            return ctx.enter_context(nc.sbuf_tensor("e_" + name, shape, dt))

        def sem(name):
            return ctx.enter_context(nc.semaphore("e_" + name))

        def banks(name, n):
            return [ctx.enter_context(nc.psum_tensor(f"e_{name}{i}", [P, 512], F32)) for i in range(n)]

        table = sb("table", [P, 3, SLOTS])
        etab, btab, newtab = [sb(name, [1, SLOTS], I32) for name in ("etab", "btab", "newtab")]
        b1T = sb("b1T", [P, E, FF // P])
        half = sb("half", [P, T])
        b1rows = sb("b1rows", [P, P])
        ident = sb("ident", [P, P])
        H_ps, Y_ps = banks("H", 4), banks("Y", 2)
        assert E * FF // P == P
        route(nc, pooled_in, wr, H_ps, table, etab, btab, newtab)

        with ExitStack() as sctx:
            b1_in, made, turned = [sctx.enter_context(nc.semaphore("e_" + n)) for n in ("b1_in", "made", "turned")]
            block = sctx.enter_context(nc.Block())

            @block.sync
            def _(sp):
                sp.dma_start(b1rows[:, :], b1.rearrange("e (t p) -> (e t) p", p=P)).then_inc(b1_in, 16)

            @block.gpsimd
            def _(pool):
                pool.memset(half[:, :], -0.5)
                pool.memset(ident[:, :], 0.0).then_inc(made, 1)
                pool.wait_ge(made, 1)
                pool.affine_select(ident[:, :], ident[:, :], [[-1, P]], ALU.not_equal, 1.0, base=0, channel_multiplier=1).then_inc(made, 1)

            @block.tensor
            def _(pe):
                pe.wait_ge(b1_in, 16)
                pe.wait_ge(made, 2)
                pe.transpose(H_ps[0][:, 0:P], b1rows[:, :], ident[:, :]).then_inc(turned, 1)

            @block.vector
            def _(dve):
                dve.wait_ge(turned, 1)
                dve.tensor_copy(b1T[:, :, :], H_ps[0][:, 0:P].rearrange("p (e t) -> p e t", e=E))

        raw = [sb(f"raw{i}", [P, 4, 512]) for i in range(RING)]
        wh = {"w1": [sb(f"w1h{c}", [P, KT, 512], F32R) for c in range(FC)], "w2": [sb(f"w2h{c}", [P, FT, D], F32R) for c in range(FC)]}
        wl = {"w1": [sb(f"w1l{c}", [P, KT, 512], F32R) for c in range(FC)], "w2": [sb(f"w2l{c}", [P, FT, D], F32R) for c in range(FC)]}
        xraw = sb("xraw", [P, KT, L])
        xh, xl = sb("xh", [P, KT, L], F32R), sb("xl", [P, KT, L], F32R)
        hf = [sb(f"hf{j}", [P, 2, L]) for j in range(2)]
        hh = [sb(f"hh{i}", [P, FT, L], F32R) for i in range(2)]
        hl = [sb(f"hl{i}", [P, FT, L], F32R) for i in range(2)]
        b1cur = sb("b1cur", [P, FF // P])
        b2cur = sb("b2cur", [P, D])
        wcur = sb("wcur", [P, 1])
        acc = sb("acc", [P, T, D])
        res = sb("res", [P, T, D])
        bn, mv, ve, rstd = sb("bn", [P, T, 6]), sb("mv", [P, T, 2]), sb("ve", [P, T]), sb("rstd", [P, T])

        names = ["x_in", "x_hi", "x_lo", "b2_in", "w_hi", "w_lo", "h_ready", "gelu_done", "h_hi", "h_lo", "y_done",
                 "b1_ready", "weight_ready", "acc_in", "acc_done", "res_done", "base_ready", "y_read", "stat", "res_ready",
                 "own_dve", "own_pool", "stood"]
        s = {n: sem(n) for n in names}
        w_in = [sem(f"w_in{i}") for i in range(RING)]
        block = ctx.enter_context(nc.Block())

        def used(n, chunk):
            kind, c = chunk
            return 8 * (n - 1) + 2 * c + 2 if kind == "w1" else FC * (n - 1) + c + 1

        def chunk_no(n, chunk):
            return 8 * n + CHUNKS.index(chunk)

        def is_new(eng, n):
            return eng.value_load(newtab[0:1, bass.ds(n, 1)], min_val=0, max_val=1)

        def slot_of(eng, n, late, rest):
            if isinstance(n, int) and n == 0:
                late(n, True)
            else:
                with eng.If(is_new(eng, n)):
                    late(n, True)
                with eng.Else():
                    late(n, False)
            if isinstance(n, int) and n == SLOTS - 1:
                rest(n, LAST3, False)
            else:
                with eng.If(is_new(eng, n + 1)):
                    rest(n, ORDER3, True)
                with eng.Else():
                    rest(n, ORDER3, False)

        @block.sync
        def _(sp):
            def load_chunk(n, e, chunk, new):
                kind, c = chunk
                k = CHUNKS.index(chunk) % RING
                sp.wait_ge(s["w_lo"], chunk_no(n, chunk) + 1)
                if not new:
                    sp.sem_inc(w_in[k], 16)
                    return
                if kind == "w1":
                    src = w1[e].rearrange("(k p) f -> p k f", p=P)[:, :, c * 512:(c + 1) * 512]
                else:
                    src = w2[e].rearrange("(c a p) d -> c p a d", a=FT, p=P)[c]
                sp.dma_start(raw[k][:, :, :], src).then_inc(w_in[k], 16)

            def load_chunks(n, e, new):
                for chunk in CHUNKS:
                    load_chunk(n, e, chunk, new)

            def slot(n):
                e = sp.value_load(etab[0:1, bass.ds(n, 1)], min_val=0, max_val=E - 1)
                b = sp.value_load(btab[0:1, bass.ds(n, 1)], min_val=0, max_val=B - 1)
                sp.wait_ge(s["x_lo"], n + 1)
                sp.dma_start(xraw[:, :, :], x2T[b + 1]).then_inc(s["x_in"], 16)
                if isinstance(n, int):
                    load_chunks(n, e, True)
                else:
                    with sp.If(is_new(sp, n)):
                        load_chunks(n, e, True)
                    with sp.Else():
                        load_chunks(n, e, False)
                sp.wait_ge(s["base_ready"], n + 1)
                sp.dma_start(b2cur[:, :], b2[e].partition_broadcast(P)).then_inc(s["b2_in"], 16)

            slot(0)
            with sp.Fori(1, SLOTS) as n:
                slot(n)

        @block.gpsimd
        def _(pool):
            def fetch_b1(n):
                e = pool.value_load(etab[0:1, bass.ds(n, 1)], min_val=0, max_val=E - 1)
                pool.wait_ge(s["gelu_done"], 8 * n + 4)
                pool.sem_inc(s["stood"], 1)
                pool.tensor_copy(b1cur[:, :], b1T[:, bass.ds(e, 1), :].rearrange("p o t -> p (o t)")).then_inc(s["b1_ready"], 1)

            def slot(n, more):
                b = pool.value_load(btab[0:1, bass.ds(n, 1)], min_val=0, max_val=B - 1)
                if not (isinstance(n, int) and n == 0):
                    stand(pool, s["acc_done"], 16 * n, s["stood"])
                pool.dma_start(acc[:, :, :], x2[b + 1].rearrange("(t p) d -> p t d", p=P)).then_inc(s["acc_in"], 16)
                pool.tensor_copy(wcur[:, :], table[:, 2, bass.ds(n, 1)]).then_inc(s["weight_ready"], 1)
                if more:
                    fetch_b1(n + 1)
                stand(pool, s["stat"], n + 1, s["stood"])
                pool.dma_start(x2[b + 1].rearrange("(t p) d -> p t d", p=P), acc[:, :, :]).then_inc(s["acc_done"], 16)
                pool.tensor_scalar(ve[:, :], mv[:, :, 1], EPS, None, ALU.add).then_inc(s["own_pool"], 1)
                pool.wait_ge(s["own_pool"], 2 * n + 1)
                pool.tensor_tensor(rstd[:, :], ve[:, :], half[:, :], ALU.pow).then_inc(s["own_pool"], 1)
                stand(pool, s["own_pool"], 2 * n + 2, s["stood"])
                if not (isinstance(n, int) and n == 0):
                    stand(pool, s["res_done"], 16 * n, s["stood"])
                for t in range(T):
                    last = pool.tensor_scalar(res[:, t, :], acc[:, t, :], mv[:, t, 0:1], rstd[:, t:t + 1], ALU.subtract, ALU.mult)
                last.then_inc(s["res_ready"], 1)
                stand(pool, s["res_ready"], n + 1, s["stood"])
                pool.dma_start(out[b].rearrange("(t p) d -> p t d", p=P), res[:, :, :]).then_inc(s["res_done"], 16)

            fetch_b1(0)
            slot(0, True)
            with pool.Fori(1, SLOTS - 1) as n:
                slot(n, True)
            slot(SLOTS - 1, False)
            pool.wait_ge(s["acc_done"], 16 * SLOTS)
            pool.wait_ge(s["res_done"], 16 * SLOTS)

        @block.scalar
        def _(act):
            act.sem_inc(s["gelu_done"], 4)

            def split(n, chunk):
                kind, c = chunk
                k = CHUNKS.index(chunk)
                act.wait_ge(w_in[k % RING], 16 * (8 // RING * n + k // RING + 1))
                act.activation(wh[kind][c][:, :, :], raw[k % RING][:, :, :], ACT.Copy).then_inc(s["w_hi"], 1)

            def hidden(n, c):
                if c == 0:
                    act.wait_ge(s["b1_ready"], n + 1)
                for j in range(2):
                    g = 2 * (FC * n + c) + j
                    act.wait_ge(s["h_ready"], g + 1)
                    act.wait_ge(s["h_lo"], g + 1)
                    for a in range(2):
                        last = act.activation(hf[j][:, a, :], H_ps[2 * (c % 2) + j][:, a * L:(a + 1) * L], ACT.Gelu,
                                              bias=b1cur[:, FT * c + 2 * j + a:FT * c + 2 * j + a + 1])
                    last.then_inc(s["gelu_done"], 1)
                for j in range(2):
                    g = 2 * (FC * n + c) + j
                    act.wait_ge(s["gelu_done"], g + 5)
                    act.activation(hh[c % 2][:, 2 * j:2 * j + 2, :], hf[j][:, :, :], ACT.Copy).then_inc(s["h_hi"], 1)

            def in_place(n, chunk):
                act.wait_ge(s["w_hi"], chunk_no(n, chunk))
                act.sem_inc(s["w_hi"], 1)

            def late(n, new):
                if not new:
                    in_place(n, LATE)
                    return
                if not (isinstance(n, int) and n == 0):
                    act.wait_ge(s["y_done"], used(n, LATE))
                split(n, LATE)

            def body(n, order, new):
                for kind, i in order:
                    if kind == "h":
                        hidden(n, i)
                    elif kind == "nh":
                        hidden(n + 1, 0)
                    elif kind == "nsplit" and not new:
                        in_place(n + 1, i)
                    elif kind == "nsplit":
                        if not (isinstance(n, int) and n == -1):
                            used_by = s["y_done"] if i[0] == "w2" else s["h_ready"]
                            act.wait_ge(used_by, used(n + 1, i))
                        split(n + 1, i)
                    elif kind == "nx":
                        if not (isinstance(n, int) and n == -1):
                            act.wait_ge(s["h_ready"], 8 * n + 8)
                        act.wait_ge(s["x_in"], 16 * (n + 2))
                        act.activation(xh[:, :, :], xraw[:, :, :], ACT.Copy).then_inc(s["x_hi"], 1)

            body(-1, FIRST3, True)
            slot_of(act, 0, late, body)
            with act.Fori(1, SLOTS - 1) as n:
                slot_of(act, n, late, body)
            slot_of(act, SLOTS - 1, late, body)

        @block.vector
        def _(dve):
            dve.sem_inc(s["w_lo"], RING)
            dve.sem_inc(s["x_lo"], 1)
            dve.sem_inc(s["h_lo"], 2)
            dve.sem_inc(s["base_ready"], 1)
            dve.sem_inc(s["y_read"], 1)

            def split(n, chunk):
                kind, c = chunk
                k = CHUNKS.index(chunk)
                dve.wait_ge(s["w_hi"], chunk_no(n, chunk) + 1)
                dve.tensor_tensor(wl[kind][c][:, :, :], raw[k % RING][:, :, :], fp(wh[kind][c][:, :, :]), ALU.subtract).then_inc(s["w_lo"], 1)

            def hidden(n, c):
                for j in range(2):
                    g = 2 * (FC * n + c) + j
                    dve.wait_ge(s["h_hi"], g + 1)
                    dve.tensor_tensor(hl[c % 2][:, 2 * j:2 * j + 2, :], hf[j][:, :, :], fp(hh[c % 2][:, 2 * j:2 * j + 2, :]),
                                      ALU.subtract).then_inc(s["h_lo"], 1)

            def in_place(n, chunk):
                dve.wait_ge(s["w_lo"], chunk_no(n, chunk) + RING)
                dve.sem_inc(s["w_lo"], 1)

            def late(n, new):
                if new:
                    split(n, LATE)
                else:
                    in_place(n, LATE)

            def body(n, order, new):
                for kind, i in order:
                    if kind == "h":
                        hidden(n, i)
                    elif kind == "nh":
                        hidden(n + 1, 0)
                    elif kind == "nsplit" and not new:
                        in_place(n + 1, i)
                    elif kind == "nsplit":
                        split(n + 1, i)
                    elif kind == "nx":
                        dve.wait_ge(s["x_hi"], n + 2)
                        dve.tensor_tensor(xl[:, :, :], xraw[:, :, :], fp(xh[:, :, :]), ALU.subtract).then_inc(s["x_lo"], 1)
                    elif kind == "base":
                        dve.wait_ge(s["acc_in"], 16 * (n + 1))
                        dve.wait_ge(s["b2_in"], 16 * (n + 1))
                        dve.wait_ge(s["weight_ready"], n + 1)
                        for t in range(T):
                            last = dve.scalar_tensor_tensor(acc[:, t, :], b2cur[:, :], wcur[:, 0:1], acc[:, t, :], ALU.mult, ALU.add)
                        last.then_inc(s["base_ready"], 1)
                    elif kind == "end":
                        dve.wait_ge(s["base_ready"], n + 2)
                        dve.wait_ge(s["y_done"], FC * (n + 1))
                        for t in range(T):
                            last = dve.scalar_tensor_tensor(acc[:, t, :], Y_ps[t][:, :], wcur[:, 0:1], acc[:, t, :], ALU.mult, ALU.add)
                        last.then_inc(s["y_read"], 1)
                        dve.wait_ge(s["y_read"], n + 2)
                        for t in range(T):
                            last = dve.bn_stats(bn[:, t, :], acc[:, t, :])
                        last.then_inc(s["own_dve"], 1)
                        stand(dve, s["own_dve"], n + 1, s["stood"])
                        for t in range(T):
                            last = dve.bn_aggr(mv[:, t, :], bn[:, t, :])
                        last.then_inc(s["stat"], 1)

            body(-1, FIRST3, True)
            slot_of(dve, 0, late, body)
            with dve.Fori(1, SLOTS - 1) as n:
                slot_of(dve, n, late, body)
            slot_of(dve, SLOTS - 1, late, body)

        @block.tensor
        def _(pe):
            def hidden(n, c):
                pe.wait_ge(s["w_lo"], chunk_no(n, ("w1", c)) + RING + 1)
                if c == 0:
                    pe.wait_ge(s["x_lo"], n + 2)
                for j in range(2):
                    g = 2 * (FC * n + c) + j
                    pe.wait_ge(s["gelu_done"], g + 1)
                    for a in range(2):
                        f = slice((2 * j + a) * P, (2 * j + a + 1) * P)
                        for k in range(KT):
                            last = product3(pe, H_ps[2 * (c % 2) + j][:, a * L:(a + 1) * L], (wh["w1"][c][:, k, f], wl["w1"][c][:, k, f]),
                                            (xh[:, k, :], xl[:, k, :]), k == 0, k == KT - 1)
                    last.then_inc(s["h_ready"], 1)

            def result(n, c):
                pe.wait_ge(s["w_lo"], chunk_no(n, ("w2", c)) + RING + 1)
                pe.wait_ge(s["h_lo"], 2 * (FC * n + c) + 4)
                if c == 0:
                    pe.wait_ge(s["y_read"], n + 1)
                for a in range(FT):
                    for t in range(T):
                        q = slice(t * P, (t + 1) * P)
                        last = product3(pe, Y_ps[t][:, :], (hh[c % 2][:, a, q], hl[c % 2][:, a, q]), (wh["w2"][c][:, a, :], wl["w2"][c][:, a, :]),
                                        c == 0 and a == 0, c == FC - 1 and a == FT - 1)
                last.then_inc(s["y_done"], 1)

            def body(n, order):
                for kind, i in order:
                    if kind == "h":
                        hidden(n, i)
                    elif kind == "nh":
                        hidden(n + 1, 0)
                    elif kind == "y":
                        result(n, i)

            body(-1, FIRST3)
            with pe.Fori(0, SLOTS - 1) as n:
                body(n, ORDER3)
            body(SLOTS - 1, LAST3)


def rope_tables():
    import numpy as np
    inv = (1.0 / np.float32(10000.0) ** (np.arange(0, D1, 2, dtype=np.float32) / np.float32(D1))).astype(np.float32)
    ang = (np.arange(L, dtype=np.float32)[:, None] * inv[None, :]).astype(np.float32).astype(np.float64)
    cos, sin = np.repeat(np.cos(ang), 2, axis=1), np.repeat(np.sin(ang), 2, axis=1)
    sin[:, 0::2] *= -1
    tab = np.stack([cos, sin]).reshape(2, T, P, D1)
    tab = np.stack([tab / np.sqrt(D1), tab])
    return np.ascontiguousarray(tab.transpose(3, 0, 1, 2, 4)).astype(np.float32)



ATTN = ["ln_gamma", "ln_beta", "Wq", "bq", "Wk", "bk", "Wv", "bv", "Wo", "bo"]
NAMES = (["x", "ctx_1024"] + ["L0_attn_" + n for n in ATTN] + ["L0_xattn_W" + c for c in "qkvo"]
         + ["L0_ffn_" + n for n in ("Wr", "W1", "b1", "W2", "b2")])


def decoder_layer(nc, a, out):
    x1 = nc.dram_tensor("x1", (B + 1, L, D), F32).ap()
    x2 = nc.dram_tensor("x2", (B + 1, L, D), F32).ap()
    x2T = nc.dram_tensor("x2T", (B + 1, P, KT, L), F32).ap()
    pooled = nc.dram_tensor("pooled", (P, KT, B + 1), F32).ap()
    with nc.sbuf_tensor("c_raw", [P, 3, KT * EMBED], F32) as raw:
        pass
    with ExitStack() as ctx:
        w_in = [ctx.enter_context(nc.semaphore(f"c_w_in{i}")) for i in range(5)]
        cross_weights = [a["L0_xattn_W" + c] for c in "qkvo"]
        ahead = [(raw[:, i, :].rearrange("p (t n) -> p t n", t=KT), cross_weights[i].rearrange("(t p) n -> p t n", p=P), w_in[i])
                 for i in range(3)]
        self_attention(nc, a["x"], a["L0_attn_ln_gamma"], a["L0_attn_ln_beta"], [a["L0_attn_W" + c] for c in "qkvo"],
                       [a["L0_attn_b" + c] for c in "qkvo"], a["rope"], x1, ahead)
        cross_attention(nc, x1, a["ctx_1024"], cross_weights, x2, x2T, pooled, raw, w_in)
    experts(nc, x2, x2T, pooled, a["L0_ffn_Wr"], a["L0_ffn_W1"], a["L0_ffn_b1"], a["L0_ffn_W2"], a["L0_ffn_b2"], out)


def kernel(**inputs):
    import numpy as _np
    import concourse.bacc as _bacc
    from concourse import mybir as _mybir
    from concourse.bass_utils import run_bass_kernel_spmd as _run

    nc = _bacc.Bacc("TRN2", target_bir_lowering=False, num_devices=1)
    given = {name: inputs[name] for name in NAMES}
    given["rope"] = rope_tables()
    arrays, a = {}, {}
    for name, value in given.items():
        value = _np.ascontiguousarray(value)
        arrays[f"in_{name}_dram"] = value
        a[name] = nc.dram_tensor(f"in_{name}_dram", value.shape, _mybir.dt.from_np(value.dtype), kind="ExternalInput").ap()
    out = nc.dram_tensor("out_0_dram", (B, L, D), F32, kind="ExternalOutput").ap()
    decoder_layer(nc, a, out)
    r = _run(nc, [arrays], core_ids=[0])
    return r.results[0]["out_0_dram"]
```
